# Optimizing a Trainium2 kernel written in Bass

```python
import numpy as np
import jax
import jax.numpy as jnp

def _softmax(x, axis=-1):
    return jax.nn.softmax(x, axis=axis)

def _gelu(x):
    return jax.nn.gelu(x, approximate=True)

def _silu(x):
    return jax.nn.silu(x)

def _sigmoid(x):
    return jax.nn.sigmoid(x)

def _layernorm(x, axis=-1, eps=1e-05):
    m = jnp.mean(x, axis=axis, keepdims=True)
    v = jnp.var(x, axis=axis, keepdims=True)
    return (x - m) / jnp.sqrt(v + eps)

def _scatter_add(tgt, idx, src, axis=0):
    return tgt.at[idx].add(src)

def _segment_sum(src, seg, n):
    return jax.ops.segment_sum(src, seg, n)
kernel_name = 'mk_adj_resnorm_d4_adj_r2_c90026'

def setup_inputs(seed: int=0):
    np.random.seed(seed)
    _w = jnp.asarray

    def _rec_inputs():
        import jax
        import jax.numpy as jnp
        _gk = jax.random.key(seed)
        x = -9.806e-05 + 1 * jax.random.normal(jax.random.fold_in(_gk, 1), (2048, 64), jnp.float32)
        _a = jax.random.bernoulli(jax.random.fold_in(_gk, 2), 0.00390625, (2048, 2048))
        _a = jnp.logical_or(_a, jnp.swapaxes(_a, -1, -2))
        _a = jnp.logical_or(_a, jnp.eye(2048, dtype=bool))
        adj = _a.astype(jnp.int32)
        return (x, adj)
    x, adj = _rec_inputs()

    def _L0_gnn_setup():
        import jax, jax.numpy as jnp
        import numpy as np
        ALPHA = 0.2
        NEG_BIG = jnp.float32(-9000000000000000.0)
        key = jax.random.key(seed)
        k1, k2, k3, k4 = jax.random.split(key, 4)
        N, F_IN, F_OUT = (4096, 64, 64)
        inputs = jax.random.normal(k1, (N, F_IN), dtype=jnp.float32)
        adj = jax.random.randint(k2, (N, N), 0, 2, dtype=jnp.int32)
        gain = 1.414
        lim_w = gain * np.sqrt(6.0 / (F_IN + F_OUT))
        W = jax.random.uniform(k3, (F_IN, F_OUT), dtype=jnp.float32, minval=-lim_w, maxval=lim_w)
        lim_a = gain * np.sqrt(6.0 / (2 * F_OUT + 1))
        a = jax.random.uniform(k4, (2 * F_OUT, 1), dtype=jnp.float32, minval=-lim_a, maxval=lim_a)
        return {'inputs': inputs, 'adj': adj, 'W': W, 'a': a}
    _L0_gnn_all = _L0_gnn_setup()
    _L0_gnn_in = {k: v for k, v in _L0_gnn_all.items() if k in ('W', 'a')}
    del _L0_gnn_all

    def _L1_gnn_setup():
        import jax, jax.numpy as jnp
        import numpy as np
        N = 2048
        OUT = 64
        EMB = 8
        K_TAYLOR = 4
        EPS = 1e-12
        key = jax.random.key(seed)
        k1, k2, k3, k4 = jax.random.split(key, 4)
        h = jax.random.normal(k1, (N, OUT), dtype=jnp.float32)
        adj = jax.random.randint(k2, (N, N), 0, 2, dtype=jnp.int32)
        w_k = jax.random.normal(k3, (OUT, EMB), dtype=jnp.float32)
        w_q = jax.random.normal(k4, (OUT, EMB), dtype=jnp.float32)
        return {'h': h, 'adj': adj, 'w_k': w_k, 'w_q': w_q}
    _L1_gnn_all = _L1_gnn_setup()
    _L1_gnn_in = {k: v for k, v in _L1_gnn_all.items() if k in ('w_k', 'w_q')}
    del _L1_gnn_all

    def _L2_gnn_setup():
        import jax, jax.numpy as jnp
        import numpy as np
        ALPHA = 0.2
        NEG_INF = -9000000000000000.0
        key = jax.random.key(seed)
        k1, k2, k3, k4 = jax.random.split(key, 4)
        N, F_IN, F_OUT = (512, 64, 64)
        h = jax.random.normal(k1, (N, F_IN), dtype=jnp.float32)
        adj = jax.random.randint(k2, (N, N), 0, 2, dtype=jnp.int32)
        lim_W = 1.414 * np.sqrt(6.0 / (F_IN + F_OUT))
        W = jax.random.uniform(k3, (F_IN, F_OUT), minval=-lim_W, maxval=lim_W, dtype=jnp.float32)
        lim_a = 1.414 * np.sqrt(6.0 / (2 * F_OUT + 1))
        a = jax.random.uniform(k4, (2 * F_OUT, 1), minval=-lim_a, maxval=lim_a, dtype=jnp.float32)
        return {'h': h, 'adj': adj, 'W': W, 'a': a}
    _L2_gnn_all = _L2_gnn_setup()
    _L2_gnn_in = {k: v for k, v in _L2_gnn_all.items() if k in ('W', 'a')}
    del _L2_gnn_all

    def _L3_gnn_setup():
        import jax, jax.numpy as jnp
        import numpy as np
        N = 4096
        F_IN = 64
        F_OUT = 64
        NEG_SLOPE = 0.01
        MASK_FILL = -1000000000000.0
        key = jax.random.key(seed)
        k1, k2, k3, k4 = jax.random.split(key, 4)
        x = jax.random.normal(k1, (N, F_IN), dtype=jnp.float32)
        adj_matrix = jax.random.randint(k2, (N, N), 0, 2, dtype=jnp.int32)
        W = jax.random.normal(k3, (F_IN, F_OUT), dtype=jnp.float32) * (1.0 / np.sqrt(F_IN))
        a = jax.random.normal(k4, (2 * F_IN, 1), dtype=jnp.float32) * (1.0 / np.sqrt(2 * F_IN))
        return {'x': x, 'adj_matrix': adj_matrix, 'W': W, 'a': a}
    _L3_gnn_all = _L3_gnn_setup()
    _L3_gnn_in = {k: v for k, v in _L3_gnn_all.items() if k in ('W', 'a')}
    del _L3_gnn_all
    return {'x': x, 'adj': adj, 'L0_gnn_W': _L0_gnn_in['W'], 'L0_gnn_a': _L0_gnn_in['a'], 'L1_gnn_w_k': _L1_gnn_in['w_k'], 'L1_gnn_w_q': _L1_gnn_in['w_q'], 'L2_gnn_W': _L2_gnn_in['W'], 'L2_gnn_a': _L2_gnn_in['a'], 'L3_gnn_W': _L3_gnn_in['W'], 'L3_gnn_a': _L3_gnn_in['a']}

def reference(x, adj, L0_gnn_W, L0_gnn_a, L1_gnn_w_k, L1_gnn_w_q, L2_gnn_W, L2_gnn_a, L3_gnn_W, L3_gnn_a):
    import jax
    import jax.numpy as jnp

    def _L0_gnn_ref(inputs, adj, W, a):
        import jax, jax.numpy as jnp
        import numpy as np
        ALPHA = 0.2
        NEG_BIG = jnp.float32(-9000000000000000.0)
        Wh = inputs @ W
        F_out = W.shape[1]
        a_src = a[:F_out, 0]
        a_dst = a[F_out:, 0]
        e = (Wh @ a_src)[:, None] + (Wh @ a_dst)[None, :]
        e = jnp.where(e > 0, e, ALPHA * e)
        scores = jnp.where(adj > 0, e, NEG_BIG)
        attention = jax.nn.softmax(scores, axis=1)
        h_prime = attention @ Wh
        return jax.nn.elu(h_prime)

    def _L1_gnn_ref(h, adj, w_k, w_q):
        import jax, jax.numpy as jnp
        import numpy as np
        N = 2048
        OUT = 64
        EMB = 8
        K_TAYLOR = 4
        EPS = 1e-12
        h = h - h.mean(axis=-1, keepdims=True)
        h = h / jnp.maximum(jnp.linalg.norm(h, axis=-1, keepdims=True), EPS)
        k = h @ w_k
        q = h @ w_q
        scores = k @ q.T / jnp.sqrt(jnp.float32(EMB))
        a_att = jax.nn.softmax(scores, axis=-1)
        a = adj.astype(jnp.float32) * a_att
        a = a / a.sum(axis=-1, keepdims=True)
        result = a
        fact = 1.0
        for i in range(2, K_TAYLOR):
            a = a @ a
            fact = fact * i
            result = result + a / fact
        return result @ h

    def _L2_gnn_ref(h, adj, W, a):
        import jax, jax.numpy as jnp
        import numpy as np
        ALPHA = 0.2
        NEG_INF = -9000000000000000.0
        F_OUT = W.shape[1]
        Wh = h @ W
        a1, a2 = (a[:F_OUT, 0], a[F_OUT:, 0])
        e = (Wh @ a1)[:, None] + (Wh @ a2)[None, :]
        e = jax.nn.leaky_relu(e, negative_slope=ALPHA)
        scores = jnp.where(adj > 0, e, jnp.float32(NEG_INF))
        attention = jax.nn.softmax(scores, axis=1)
        h_prime = attention @ Wh
        return jax.nn.elu(h_prime)

    def _L3_gnn_ref(x, adj_matrix, W, a):
        import jax, jax.numpy as jnp
        import numpy as np
        N = 4096
        F_IN = 64
        F_OUT = 64
        NEG_SLOPE = 0.01
        MASK_FILL = -1000000000000.0
        h = x @ W
        a1 = a[:F_OUT, 0]
        a2 = a[F_OUT:, 0]
        f1 = h @ a1
        f2 = h @ a2
        e = jax.nn.leaky_relu(f1[:, None] + f2[None, :], NEG_SLOPE)
        e = jnp.where(adj_matrix > 0, e, MASK_FILL)
        attention = jax.nn.softmax(e, axis=1)
        h_prime = attention @ h
        return jax.nn.elu(h_prime)
    x = _layernorm(x + _L0_gnn_ref(x, adj, L0_gnn_W, L0_gnn_a), axis=-1)
    x = _layernorm(x + _L1_gnn_ref(x, adj, L1_gnn_w_k, L1_gnn_w_q), axis=-1)
    x = _layernorm(x + _L2_gnn_ref(x, adj, L2_gnn_W, L2_gnn_a), axis=-1)
    x = _layernorm(x + _L3_gnn_ref(x, adj, L3_gnn_W, L3_gnn_a), axis=-1)
    return x

_drawn_inputs = setup_inputs


def setup_inputs(seed=0):
    import zlib

    import numpy as np

    out = dict(_drawn_inputs(seed))
    spreads = {}
    factors = {}
    for name, (base, spread) in spreads.items():
        noise = np.random.default_rng([zlib.crc32(name.encode()), seed]).standard_normal(out[name].shape)
        drawn = base * np.exp(spread * noise) if base else spread * noise
        out[name] = jnp.asarray(drawn.astype(out[name].dtype))
    for name, factor in factors.items():
        out[name] = (out[name] * factor).astype(out[name].dtype)
    return out
```

```python
from contextlib import ExitStack

import concourse.bass as bass
from concourse import mybir

ALU = mybir.AluOpType
ACT = mybir.ActivationFunctionType
F32 = mybir.dt.float32
BF16 = mybir.dt.bfloat16
U8 = mybir.dt.uint8
AX_X = mybir.AxisListType.X


def graph_layers(nc, x_in, adj_in, weights_in, out, slopes):
    PART = 128
    F = 64
    N = x_in.shape[1] // F * PART
    NT = N // PART
    GT = 4
    NG = NT // GT
    GW = GT * PART
    FV = F + 1
    E = 8
    NL = 3
    LW = 2 * F + 2
    STACK = 9 * E
    STACKM = STACK + 3
    SCORE_SCALE = 1.0 / float(E) ** 0.5
    LN_EPS = 1e-5
    NORM_SCALE = 2.0 ** 40
    LN_BOUND = 2.0801
    HALF_LN_SCALE = 0.5 * 40 * 0.6931471805599453

    with ExitStack() as ctx:
        def sb(name, shape, dt):
            return ctx.enter_context(nc.sbuf_tensor(name, shape, dt))

        def sem(name):
            return ctx.enter_context(nc.semaphore(name))

        adj = sb("adj", [PART, NG, NT, GW], U8)
        prob = sb("prob", [PART, NG, NT, GW], F32)
        x = sb("x", [PART, NT, F], F32)
        y = sb("y", [PART, NT, F], F32)
        val = sb("val", [PART, 2, NT, FV], F32)
        wts = sb("wts", [F, NL * LW + 2 * E], F32)
        a_rep = [prob[0:F, 0, al, 0:PART + 2] for al in range(NL)]
        w_src = sb("w_src", [F, NL, PART], F32)
        w_ext = sb("w_ext", [F, NL, F + 2], F32)
        w_dst2 = sb("w_dst2", [F, NL], F32)
        ident = sb("ident", [PART, PART], F32)
        identb = sb("identb", [PART, PART], BF16)
        ones = sb("ones", [F, PART], F32)
        cst = sb("cst", [PART, 4], F32)
        xT = sb("xT", [F, NG, GW], F32)
        r_row = sb("r_row", [PART, NG, GW], F32)
        stackT = r_row[:, :, :].rearrange("p g i -> p (g i)").bitcast(BF16).rearrange("p (w g i) -> p w g i", w=2, g=NG)
        kT, qT = stackT[0:STACKM, 0], stackT[0:STACKM, 1]
        d_col = sb("d_col", [PART, NT], F32)
        b_col = sb("b_col", [PART, 2, NT], F32)
        dmax = sb("dmax", [PART, 1], F32)
        dmax1 = sb("dmax1", [1, 1], F32)
        shift = sb("shift", [PART, NL, 4], F32)
        ln_norm = sb("ln_norm", [PART, NL], F32)
        rinv = sb("rinv", [PART, NT], F32)
        h = sb("h", [PART, 2, GT, F], F32)
        e = sb("e", [PART, 2, GT, F], F32)
        stats = sb("stats", [PART, 2, GT, 6], F32)
        mv = sb("mv", [PART, 2, GT, 2], F32)
        v, lnv, r0, sq, vsq, corr, rstd = (sb(n, [PART, 2, GT], F32) for n in
                                           ("v", "lnv", "r0", "sq", "vsq", "corr", "rstd"))
        kq = sb("kq", [PART, 3, GT, 2 * E], F32)
        kq_part = sb("kq_part", [PART, 3, GT, 2 * E], BF16)
        k_stack = sb("k_stack", [PART, NT, STACKM], BF16)
        q_stack = y[:, :, :].bitcast(BF16)[:, :, 0:STACKM]
        mx = sb("mx", [PART, 3, NT], F32)

        psum = ctx.enter_context(nc.psum_tensor("psum", [PART, 8, 512], F32))
        TR, SRC, WH, MISC = 4, 5, 6, 7

        def acc(b):
            return psum[:, b, 0:GT * FV].rearrange("p (t f) -> p t f", f=FV)

        def wh(b):
            return psum[:, b, 0:GT * (F + 2)].rearrange("p (t f) -> p t f", f=F + 2)

        def tiles(g):
            return slice(g * GT, (g + 1) * GT)

        SLOT = [0, 1, 0]

        x_loaded = sem("x_loaded")
        w_loaded = sem("w_loaded")
        adj_loaded = [sem(f"adj_loaded{n}") for n in range(NG * 4)]
        stored = sem("stored")
        zeroed = sem("zeroed")
        ident_ready = sem("ident_ready")
        consts_ready = sem("consts_ready")
        arep_ready = sem("arep_ready")
        wa_done = sem("wa_done")
        wcopy_ready = sem("wcopy_ready")
        wsq_ready = sem("wsq_ready")
        wnorm_done = sem("wnorm_done")
        lnnorm_ready = sem("lnnorm_ready")
        bound_ready = sem("bound_ready")
        dmax_part = sem("dmax_part")
        dmax_turned = sem("dmax_turned")
        dmax_one = sem("dmax_one")
        dmax_spread = sem("dmax_spread")
        dmax_ready = sem("dmax_ready")
        shift_ready = sem("shift_ready")
        tr_done = sem("tr_done")
        xT_ready = sem("xT_ready")
        wh_done = sem("wh_done")
        src_done = sem("src_done")
        d_ready = sem("d_ready")
        relu_ready = sem("relu_ready")
        r_ready = sem("r_ready")
        b_ready = sem("b_ready")
        weight_ready = sem("weight_ready")
        val_ready = sem("val_ready")
        p_ready = sem("p_ready")
        acc_done = sem("acc_done")
        rinv_ready = sem("rinv_ready")
        h_ready = sem("h_ready")
        neg_ready = sem("neg_ready")
        e_ready = sem("e_ready")
        y0_ready = sem("y0_ready")
        y_ready = sem("y_ready")
        stats_ready = sem("stats_ready")
        mv_ready = sem("mv_ready")
        v_ready = sem("v_ready")
        lnv_ready = sem("lnv_ready")
        r0_ready = sem("r0_ready")
        newton = sem("newton")
        x_ready = sem("x_ready")
        hn_ready = sem("hn_ready")
        kq_done = sem("kq_done")
        kq_step = sem("kq_step")
        stacks_ready = sem("stacks_ready")
        stackT_done = sem("stackT_done")
        stackT_ready = sem("stackT_ready")
        max_scores = sem("max_scores")
        mx_ready = sem("mx_ready")
        m_step = sem("m_step")
        mT_done = sem("mT_done")
        mT_ready = sem("mT_ready")
        scores_done = sem("scores_done")
        exp_done = sem("exp_done")
        pa_ready = sem("pa_ready")
        va_done = sem("va_done")
        va_rinv = sem("va_rinv")
        va_ready = sem("va_ready")
        res_ready = sem("res_ready")

        def norm_at(layer, g):
            if layer == 0:
                return 2 * g
            if layer == "h":
                return 2 * g + 1
            return 2 * NG + (layer - 1) * NG + g

        def turn_at(al, g):
            return {0: 0, "h": 1, 1: 2, 2: 3}[al] * NG + g

        LAYER = [0, 2, 3]
        TERM = [1.0, 0.5, 0.0, 1.0 / 6.0]

        block = ctx.enter_context(nc.Block())

        @block.sync
        def _(sp):
            sp.dma_start(x[:, :, :], x_in.rearrange("p (t f) -> p t f", f=F)).then_inc(x_loaded, 16)
            sp.dma_start(wts[:, :], weights_in).then_inc(w_loaded, 16)
            for g in range(NG):
                sp.wait_ge(x_ready, 3 * NG + g + 1)
                sp.dma_start(out[:, g * GT * F:(g + 1) * GT * F],
                             x[:, tiles(g), :].rearrange("p t f -> p (t f)")).then_inc(stored, 16)
            sp.wait_ge(stored, 16 * NG)

        def norm_pool(pool, i, is_h):
            b = i % 2
            pool.wait_ge(mv_ready, i + 1)
            if is_h:
                pool.tensor_scalar(v[:, b, :], mv[:, b, :, 1], float(F), 1e-24, ALU.mult, ALU.max).then_inc(v_ready, 1)
            else:
                pool.tensor_scalar(v[:, b, :], mv[:, b, :, 1], LN_EPS, None, ALU.add).then_inc(v_ready, 1)
            pool.wait_ge(r0_ready, i + 1)
            pool.tensor_tensor(sq[:, b, :], r0[:, b, :], r0[:, b, :], ALU.mult).then_inc(newton, 1)
            pool.wait_ge(newton, 4 * i + 1)
            pool.tensor_tensor(vsq[:, b, :], sq[:, b, :], v[:, b, :], ALU.mult).then_inc(newton, 1)
            pool.wait_ge(newton, 4 * i + 2)
            pool.tensor_scalar(corr[:, b, :], vsq[:, b, :], -0.5, 1.5, ALU.mult, ALU.add).then_inc(newton, 1)
            pool.wait_ge(newton, 4 * i + 3)
            pool.tensor_tensor(rstd[:, b, :], corr[:, b, :], r0[:, b, :], ALU.mult).then_inc(newton, 1)

        @block.gpsimd
        def _(pool):
            pool.memset(ident[:, :], 0.0).then_inc(zeroed, 1)
            for g in range(NG):
                for c in range(4):
                    pool.dma_start(adj[:, g, 4 * c:4 * c + 4, :],
                                   adj_in[g, :, 4 * c * GW:(4 * c + 4) * GW].rearrange("p (t i) -> p t i", i=GW),
                                   max_dma_last_dim=8192).then_inc(adj_loaded[4 * g + c], 16)
                    if g == 0 and c == 0:
                        pool.wait_ge(zeroed, 1)
                        pool.affine_select(out=ident[:, :], in_=ident[:, :], compare_op=ALU.not_equal, fill=1.0,
                                           base=0, pattern=[[-1, PART]], channel_multiplier=1).then_inc(ident_ready, 1)
            for g in range(NG):
                norm_pool(pool, norm_at(0, g), False)
                norm_pool(pool, norm_at("h", g), True)
            for layer in range(1, 4):
                for g in range(NG):
                    norm_pool(pool, norm_at(layer, g), False)

        def turned_act(act, n, g):
            act.wait_ge(tr_done, n + 1)
            act.activation(xT[:, g, :], psum[0:F, TR, :], ACT.Copy).then_inc(xT_ready, 1)

        def weights_act(act, al, g):
            k = al * NG + g
            act.wait_ge(shift_ready, 3 * (al + 1))
            act.wait_ge(d_ready, k + 1)
            act.activation(b_col[:, al % 2, tiles(g)], d_col[:, tiles(g)], ACT.Exp, bias=shift[:, al, 2:3],
                           scale=1.0 - slopes[al]).then_inc(b_ready, 1)
            act.activation(val[:, SLOT[al], tiles(g), F], d_col[:, tiles(g)], ACT.Exp, bias=shift[:, al, 3:4],
                           scale=slopes[al]).then_inc(weight_ready, 1)

        def row_act(act, al, g):
            k = al * NG + g
            act.wait_ge(src_done, k + 1)
            act.activation(r_row[:, g, :], psum[:, SRC, :], ACT.Relu, bias=shift[:, al, 1:2],
                           scale=1.0 - slopes[al]).then_inc(relu_ready, 1)
            act.wait_ge(relu_ready, k + 1)
            act.activation(r_row[:, g, :], r_row[:, g, :], ACT.Exp, scale=-1.0).then_inc(r_ready, 1)

        def elu_act(act, al, g):
            k = al * NG + g
            act.wait_ge(h_ready, k + 1)
            act.activation(e[:, k % 2], h[:, k % 2], ACT.Relu, scale=-1.0).then_inc(neg_ready, 1)
            act.wait_ge(neg_ready, k + 1)
            act.activation(e[:, k % 2], e[:, k % 2], ACT.Exp, scale=-1.0).then_inc(e_ready, 1)

        def norm_act(act, i, is_h):
            b = i % 2
            act.wait_ge(v_ready, i + 1)
            act.activation(lnv[:, b, :], v[:, b, :], ACT.Ln, scale=NORM_SCALE if is_h else 1.0).then_inc(lnv_ready, 1)
            act.wait_ge(lnv_ready, i + 1)
            act.activation(r0[:, b, :], lnv[:, b, :], ACT.Exp, scale=-0.5,
                           bias=cst[:, 1:2] if is_h else cst[:, 0:1]).then_inc(r0_ready, 1)

        def next_inputs_act(act, al, g):
            turned_act(act, turn_at(al, g), g)
            weights_act(act, al, g)
            row_act(act, al, g)

        def layer1_act(act):
            for g in range(NG):
                for which, dst in ((0, kT), (1, qT)):
                    act.wait_ge(stackT_done, 2 * g + which + 1)
                    act.activation(dst[0:STACKM, g, :], turned_stack(which), ACT.Copy).then_inc(stackT_ready, 1)
            for g in range(NG):
                act.wait_ge(mT_done, g + 1)
                act.activation(kT[0:STACKM, g, :], turned_stack(g % 2), ACT.Copy).then_inc(mT_ready, 1)
            for n in range(NG * NT // 2):
                act.wait_ge(scores_done, n + 1)
                pair = psum[:, 2 + 2 * (n % 3):4 + 2 * (n % 3), :]
                act.activation(pair, pair, ACT.Exp, scale=SCORE_SCALE).then_inc(exp_done, 1)
            for g in range(NG):
                norm_act(act, norm_at(1, g), False)
                next_inputs_act(act, 1, g)

        def turned_stack(which):
            return psum[0:STACKM, [SRC, MISC][which], :].bitcast(BF16)[:, 0:GW]

        @block.scalar
        def _(act):
            act.wait_ge(consts_ready, 1)
            for g in range(NG):
                turned_act(act, turn_at(0, g), g)
            act.wait_ge(wnorm_done, 1)
            act.activation(ln_norm[:, 1:NL], psum[:, MISC, 256:256 + NL - 1], ACT.Ln, bias=cst[:, 2:3]).then_inc(lnnorm_ready, 1)
            act.wait_ge(lnnorm_ready, 1)
            act.activation(shift[:, 1:NL, 0], ln_norm[:, 1:NL], ACT.Exp, scale=0.5, bias=cst[:, 3:4]).then_inc(bound_ready, 1)
            for g in range(NG):
                weights_act(act, 0, g)
            for g in range(NG):
                row_act(act, 0, g)
            for al in range(NL):
                for g in range(NG):
                    elu_act(act, al, g)
                    norm_act(act, norm_at(LAYER[al], g), False)
                    if al == 0:
                        norm_act(act, norm_at("h", g), True)
                        turned_act(act, turn_at("h", g), g)
                    if al == 1:
                        next_inputs_act(act, 2, g)
                if al == 0:
                    layer1_act(act)

        def block_dve(dve, al, g, jt):
            if jt == 0:
                dve.wait_ge(r_ready, al * NG + g + 1)
                if al == 1:
                    dve.wait_ge(va_done, 3 * NG + g + 1)
                if al == 2:
                    dve.wait_ge(acc_done, NG + g + 1)
            if jt % GT == 0:
                dve.wait_ge(b_ready, al * NG + jt // GT + 1)
                if al == 0:
                    dve.wait_ge(adj_loaded[4 * g + jt // 4], 16)
            dve.scalar_tensor_tensor(out=prob[:, g, jt, :], in0=r_row[:, g, :], scalar=b_col[:, al % 2, jt:jt + 1],
                                     in1=adj[:, g, jt, :], op0=ALU.max, op1=ALU.mult).then_inc(p_ready, 1)

        def elu_dve(dve, al, g, step):
            k = al * NG + g
            b = k % 2
            a = acc(g)
            if step == 0:
                dve.wait_ge(acc_done, k + 1)
                dve.reciprocal(rinv[:, tiles(g)], a[:, :, F]).then_inc(rinv_ready, 1)
            if step == 1:
                dve.wait_ge(rinv_ready, k + 1)
                dve.tensor_tensor(h[:, b], a[:, :, 0:F], rinv[:, tiles(g)].unsqueeze(2).to_broadcast([PART, GT, F]),
                                  ALU.mult).then_inc(h_ready, 1)
            if step == 2:
                dve.wait_ge(h_ready, k + 1)
                dve.scalar_tensor_tensor(out=y[:, tiles(g), :], in0=h[:, b], scalar=0.0, in1=x[:, tiles(g), :],
                                         op0=ALU.max, op1=ALU.add).then_inc(y0_ready, 1)
            if step == 3:
                dve.wait_ge(e_ready, k + 1)
                dve.wait_ge(y0_ready, k + 1)
                dve.scalar_tensor_tensor(out=y[:, tiles(g), :], in0=e[:, b], scalar=-1.0, in1=y[:, tiles(g), :],
                                         op0=ALU.add, op1=ALU.add).then_inc(y_ready, 1)

        def norm_dve(dve, i, g, step, src, dst, given, count, done):
            b = i % 2
            if step == 0:
                dve.wait_ge(given, count)
                for q in range(GT):
                    last = dve.bn_stats(stats[:, b, q, :], src[:, g * GT + q, 0:F])
                last.then_inc(stats_ready, 1)
            if step == 1:
                dve.wait_ge(stats_ready, i + 1)
                for q in range(GT):
                    last = dve.bn_aggr(mv[:, b, q, :], stats[:, b, q, :])
                last.then_inc(mv_ready, 1)
            if step == 2:
                dve.wait_ge(mv_ready, i + 1)
                dve.wait_ge(newton, 4 * (i + 1))
                for q in range(GT):
                    last = dve.tensor_scalar(dst[:, g * GT + q, 0:F], src[:, g * GT + q, 0:F], mv[:, b, q, 0:1],
                                             rstd[:, b, q:q + 1], ALU.subtract, ALU.mult)
                last.then_inc(done, 1)

        def layer_norm_dve(dve, layer, g, step):
            norm_dve(dve, norm_at(layer, g), g, step, y, x, y_ready, layer * NG + g + 1, x_ready)

        def d_dve(dve, al, g):
            dve.wait_ge(wh_done, al * NG + g + 1)
            dve.tensor_copy(d_col[:, tiles(g)], wh(g if al == 0 else WH)[:, :, F + 1]).then_inc(d_ready, 1)

        def values_dve(dve, al, g):
            dve.wait_ge(weight_ready, al * NG + g + 1)
            v_g = val[:, SLOT[al], tiles(g), :]
            dve.tensor_tensor(v_g[:, :, 0:F], wh(g if al == 0 else WH)[:, :, 0:F],
                              v_g[:, :, F:F + 1].to_broadcast([PART, GT, F]), ALU.mult).then_inc(val_ready, 1)

        def keys_dve(dve, g):
            src = psum[:, WH, 0:GT * 2 * E].rearrange("p (t f) -> p t f", f=2 * E)
            dve.wait_ge(kq_done, g + 1)
            n = 6 * g
            dve.tensor_copy(kq[:, 0], src).then_inc(kq_step, 1)
            for a in range(3):
                n += 1
                dve.wait_ge(kq_step, n)
                dve.tensor_copy(kq_part[:, a], kq[:, a]).then_inc(kq_step, 1)
                if a < 2:
                    n += 1
                    dve.wait_ge(kq_step, n)
                    dve.tensor_tensor(kq[:, a + 1], kq[:, a], kq_part[:, a], ALU.subtract).then_inc(kq_step, 1)
            dve.wait_ge(kq_step, n + 1)
            ks = k_stack[:, tiles(g), 0:STACK].rearrange("p t (a c e) -> p t a c e", a=3, c=3)
            qs = q_stack[:, tiles(g), 0:STACK].rearrange("p t (a c e) -> p t a c e", a=3, c=3)
            for a in range(3):
                dve.tensor_copy(ks[:, :, a, :, :], kq_part[:, a, :, 0:E].unsqueeze(2).to_broadcast([PART, GT, 3, E]))
                last = dve.tensor_copy(qs[:, :, :, a, :],
                                       kq_part[:, a, :, E:2 * E].unsqueeze(2).to_broadcast([PART, GT, 3, E]))
            last = dve.memset(q_stack[:, tiles(g), STACK:STACKM], 1.0)
            last.then_inc(stacks_ready, 1)

        def group_step_dve(dve, al, g, jt):
            if jt < 4:
                elu_dve(dve, al, g, jt)
            if jt in (4, 5, 8):
                layer_norm_dve(dve, LAYER[al], g, {4: 0, 5: 1, 8: 2}[jt])
            if al == 0 and jt in (9, 10, 13):
                norm_dve(dve, norm_at("h", g), g, {9: 0, 10: 1, 13: 2}[jt], x, val[:, 1], x_ready, g + 1, hn_ready)
            if al == 0 and jt == 15:
                keys_dve(dve, g)
            if al == 1 and jt == 10:
                d_dve(dve, 2, g)
            if al == 1 and jt == 11:
                values_dve(dve, 2, g)

        def product_dve(dve, n, g):
            k = n * NG + g
            a = acc(k % 2)
            dst = val[:, n % 2, tiles(g), 0:F]
            dve.wait_ge(va_done, k + 1)
            if n == 0:
                dve.reciprocal(rinv[:, tiles(g)], a[:, :, F]).then_inc(va_rinv, 1)
                dve.wait_ge(va_rinv, g + 1)
            dve.tensor_tensor(dst, a[:, :, 0:F], rinv[:, tiles(g)].unsqueeze(2).to_broadcast([PART, GT, F]),
                              ALU.mult).then_inc(va_ready, 1)
            if n == 2:
                return
            before = x if n == 0 else y
            dve.wait_ge(va_ready, k + 1)
            if n > 0:
                dve.wait_ge(res_ready, (NG if n == 3 else 0) + g + 1)
            dve.scalar_tensor_tensor(out=y[:, tiles(g), :], in0=dst, scalar=TERM[n], in1=before[:, tiles(g), :],
                                     op0=ALU.mult, op1=ALU.add).then_inc(y_ready if n == 3 else res_ready, 1)

        def layer1_dve(dve):
            for i in range(NT):
                dve.wait_ge(max_scores, i + 1)
                dve.tensor_reduce(mx[:, 0, i:i + 1], psum[:, 4 * (i % 2):4 * (i % 2) + 4, :], mybir.AxisListType.XY,
                                  ALU.max, negate=True).then_inc(mx_ready, 1)
            dve.wait_ge(mx_ready, NT)
            for a in range(3):
                if a:
                    dve.wait_ge(m_step, 2 * a)
                dve.tensor_copy(k_stack[:, :, STACK + a], mx[:, a, :]).then_inc(m_step, 1)
                if a < 2:
                    dve.wait_ge(m_step, 2 * a + 1)
                    dve.tensor_tensor(mx[:, a + 1, :], mx[:, a, :], k_stack[:, :, STACK + a],
                                      ALU.subtract).then_inc(m_step, 1)
            for g in range(NG):
                for c in range(NT // 2):
                    n = g * NT // 2 + c
                    dve.wait_ge(exp_done, n + 1)
                    dve.tensor_tensor(prob[:, g, 2 * c:2 * c + 2, :], psum[:, 2 + 2 * (n % 3):4 + 2 * (n % 3), :],
                                      adj[:, g, 2 * c:2 * c + 2, :], ALU.mult).then_inc(pa_ready, 1)
                    if g > 0 and c == 3:
                        product_dve(dve, 0, g - 1)
            product_dve(dve, 0, NG - 1)
            for n in range(1, 4):
                for g in range(NG):
                    product_dve(dve, n, g)
                    if n == 3:
                        for step in range(3):
                            layer_norm_dve(dve, 1, g, step)
                        d_dve(dve, 1, g)
                        values_dve(dve, 1, g)

        @block.vector
        def _(dve):
            dve.memset(ones[:, :], 1.0)
            dve.memset(cst[:, 0:1], 0.0)
            dve.memset(cst[:, 1:2], HALF_LN_SCALE)
            dve.memset(cst[:, 2:3], 1e-12)
            dve.memset(cst[:, 3:4], LN_BOUND)
            dve.memset(val[:, 1, :, F:FV], 1.0)
            dve.memset(k_stack[:, :, STACK:STACKM], 0.0).then_inc(consts_ready, 1)
            dve.wait_ge(w_loaded, 16)
            for al in range(NL):
                o = al * LW + 2 * F
                dve.tensor_copy(w_ext[:, al, 0:F], wts[:, al * LW:al * LW + F])
                dve.tensor_copy(a_rep[al][:, 0:PART], wts[:, o:o + 1].to_broadcast([F, PART]))
                last = dve.tensor_copy(a_rep[al][:, PART:PART + 2], wts[:, o:o + 2])
            last.then_inc(arep_ready, 1)
            dve.wait_ge(wa_done, 1)
            for al in range(NL):
                wa = psum[0:F, 5 + al, 0:PART + 2]
                dve.tensor_copy(w_src[:, al, :], wa[:, 0:PART])
                last = dve.tensor_copy(w_ext[:, al, F:F + 2], wa[:, PART:PART + 2])
            last.then_inc(wcopy_ready, 1)
            dve.wait_ge(wcopy_ready, 1)
            dve.tensor_tensor(w_dst2[:, :], w_ext[:, :, F + 1], w_ext[:, :, F + 1], ALU.mult).then_inc(wsq_ready, 1)
            dve.wait_ge(ident_ready, 1)
            dve.tensor_copy(identb[:, :], ident[:, :]).then_inc(consts_ready, 1)
            for g in range(NG):
                d_dve(dve, 0, g)
            dve.wait_ge(d_ready, NG)
            dve.tensor_reduce(dmax[:, :], d_col[:, :], AX_X, ALU.max).then_inc(dmax_part, 1)
            dve.wait_ge(dmax_turned, 1)
            dve.tensor_reduce(dmax1[:, :], psum[0:1, MISC, 0:PART], AX_X, ALU.max).then_inc(dmax_one, 1)
            dve.wait_ge(dmax_spread, 1)
            dve.tensor_copy(shift[:, 0, 0:1], psum[:, MISC, 384:385]).then_inc(dmax_ready, 1)
            dve.wait_ge(dmax_ready, 1)
            for al in range(NL):
                if al == 1:
                    dve.wait_ge(bound_ready, 1)
                c = shift[:, al, 0:1]
                dve.tensor_scalar(shift[:, al, 1:2], c, 1.0 - slopes[al], None, ALU.mult).then_inc(shift_ready, 1)
                dve.tensor_scalar(shift[:, al, 2:3], c, slopes[al] - 1.0, None, ALU.mult).then_inc(shift_ready, 1)
                dve.tensor_scalar(shift[:, al, 3:4], c, -slopes[al], None, ALU.mult).then_inc(shift_ready, 1)
            for g in range(NG):
                values_dve(dve, 0, g)
            for al in range(NL):
                for g in range(NG):
                    for jt in range(NT):
                        block_dve(dve, al, g, jt)
                        if g > 0:
                            group_step_dve(dve, al, g - 1, jt)
                        elif al == 2:
                            group_step_dve(dve, 1, NG - 1, jt)
                if al != 1:
                    for jt in range(NT):
                        group_step_dve(dve, al, NG - 1, jt)
                if al == 0:
                    layer1_dve(dve)

        def turn_pe(pe, n, src, g, given, count):
            pe.wait_ge(given, count)
            if n > 0:
                pe.wait_ge(xT_ready, n)
            for q in range(GT):
                last = pe.transpose(psum[0:F, TR, q * PART:(q + 1) * PART], src[:, g * GT + q, 0:F], ident[:, :])
            last.then_inc(tr_done, 1)

        def wh_pe(pe, al, g):
            k = al * NG + g
            pe.wait_ge(xT_ready, turn_at(al, g) + 1)
            if al > 0 and g > 0:
                pe.wait_ge(val_ready, k)
            for q in range(GT):
                last = pe.matmul(wh(g if al == 0 else WH)[:, q, :], xT[:, g, q * PART:(q + 1) * PART], w_ext[:, al, :],
                                 start=(q == 0), stop=(q == GT - 1), skip_group_check=True)
            last.then_inc(wh_done, 1)

        def src_pe(pe, al, g):
            k = al * NG + g
            if k > 0:
                pe.wait_ge(relu_ready, k)
            pe.matmul(psum[:, SRC, :], w_src[:, al, :], xT[:, g, :], start=True, stop=True).then_inc(src_done, 1)

        def group_pe(pe, al, g):
            if al == 0:
                turn_pe(pe, turn_at("h", g), val[:, 1], g, hn_ready, g + 1)
                pe.wait_ge(xT_ready, turn_at("h", g) + 1)
                if g > 0:
                    pe.wait_ge(stacks_ready, g)
                for q in range(GT):
                    last = pe.matmul(psum[:, WH, q * 2 * E:(q + 1) * 2 * E], xT[:, g, q * PART:(q + 1) * PART],
                                     wts[:, NL * LW:NL * LW + 2 * E], start=(q == 0), stop=(q == GT - 1),
                                     skip_group_check=True)
                last.then_inc(kq_done, 1)
            if al == 1:
                turn_pe(pe, turn_at(2, g), x, g, x_ready, 2 * NG + g + 1)
                wh_pe(pe, 2, g)
                src_pe(pe, 2, g)

        def group_sums_pe(pe, al, g):
            for jt in range(NT):
                pe.wait_ge(p_ready, (al * NG + g) * NT + jt + 1)
                if jt % GT == 0:
                    pe.wait_ge(val_ready, al * NG + jt // GT + 1)
                if jt == 0 and al == 0:
                    pe.wait_ge(val_ready, NG)
                if jt == 0 and al == 1:
                    pe.wait_ge(va_ready, 4 * NG)
                if jt == 0 and al == 2:
                    pe.wait_ge(h_ready, NG + g + 1)
                for q in range(GT):
                    last = pe.matmul(acc(g)[:, q, :], prob[:, g, jt, q * PART:(q + 1) * PART], val[:, SLOT[al], jt, :],
                                     start=(jt == 0 and q == 0), stop=(jt == NT - 1 and q == GT - 1),
                                     skip_group_check=True)
                if jt == (13 if al == 0 else 8):
                    if g > 0:
                        group_pe(pe, al, g - 1)
                    elif al == 2:
                        group_pe(pe, 1, NG - 1)
            last.then_inc(acc_done, 1)

        def turn_stack_pe(pe, which, g, stack):
            for q in range(GT):
                last = pe.transpose(turned_stack(which)[:, q * PART:(q + 1) * PART], stack[:, g * GT + q, :], identb[:, :])
            return last

        def layer1_pe(pe):
            for g in range(NG):
                pe.wait_ge(stacks_ready, g + 1)
                if g == 0:
                    pe.wait_ge(relu_ready, NG)
                for which, stack in ((0, k_stack), (1, q_stack)):
                    if g > 0:
                        pe.wait_ge(stackT_ready, 2 * g - 1 + which)
                    turn_stack_pe(pe, which, g, stack).then_inc(stackT_done, 1)
            pe.wait_ge(stackT_ready, 2 * NG)
            for i in range(NT):
                if i == 0:
                    pe.wait_ge(h_ready, NG)
                if i > 1:
                    pe.wait_ge(mx_ready, i - 1)
                for c in range(NG):
                    last = pe.matmul(psum[:, 4 * (i % 2) + c, :], kT[0:STACK, i // GT, (i % GT) * PART:(i % GT + 1) * PART],
                                     qT[0:STACK, c, :], start=True, stop=True)
                last.then_inc(max_scores, 1)
            for g in range(NG):
                pe.wait_ge(m_step, 5)
                if g > 1:
                    pe.wait_ge(mT_ready, g - 1)
                turn_stack_pe(pe, g % 2, g, k_stack).then_inc(mT_done, 1)
            pe.wait_ge(mT_ready, NG)
            for g in range(NG):
                for c in range(NT // 2 + 2):
                    if c < NT // 2:
                        n = g * NT // 2 + c
                        if n > 2:
                            pe.wait_ge(pa_ready, n - 2)
                        for a in range(2):
                            jt = 2 * c + a
                            last = pe.matmul(psum[:, 2 + 2 * (n % 3) + a, :],
                                             qT[:, jt // GT, (jt % GT) * PART:(jt % GT + 1) * PART], kT[:, g, :],
                                             start=True, stop=True)
                        last.then_inc(scores_done, 1)
                    if c >= 2:
                        pe.wait_ge(pa_ready, g * NT // 2 + c - 1)
                        if c == 2 and g > 1:
                            pe.wait_ge(va_ready, g - 1)
                        for a in range(2):
                            jt = 2 * (c - 2) + a
                            for q in range(GT):
                                last = pe.matmul(acc(g % 2)[:, q, :], prob[:, g, jt, q * PART:(q + 1) * PART],
                                                 val[:, 1, jt, :], start=(jt == 0 and q == 0),
                                                 stop=(jt == NT - 1 and q == GT - 1), skip_group_check=True)
                last.then_inc(va_done, 1)
            for n in range(1, 4):
                for g in range(NG):
                    k = n * NG + g
                    pe.wait_ge(va_ready, k - 1)
                    for q in range(GT):
                        for jt in range(NT):
                            if g == 0 and q == 0 and jt % GT == 0:
                                pe.wait_ge(va_ready, (n - 1) * NG + jt // GT + 1)
                            last = pe.matmul(acc(k % 2)[:, q, 0:F], prob[:, g, jt, q * PART:(q + 1) * PART],
                                             val[:, (n + 1) % 2, jt, 0:F], start=(jt == 0 and q == 0),
                                             stop=(jt == NT - 1 and q == GT - 1), skip_group_check=True)
                    last.then_inc(va_done, 1)
                    if n == 3 and g > 0:
                        inputs_pe(pe, 1, g - 1)
            inputs_pe(pe, 1, NG - 1)

        def inputs_pe(pe, al, g):
            turn_pe(pe, turn_at(al, g), x, g, x_ready, NG * (LAYER[al] - 1) + g + 1)
            wh_pe(pe, al, g)
            src_pe(pe, al, g)

        @block.tensor
        def _(pe):
            pe.wait_ge(arep_ready, 1)
            pe.wait_ge(w_loaded, 16)
            for al in range(NL):
                last = pe.matmul(psum[0:F, 5 + al, 0:PART + 2], wts[:, al * LW + F:al * LW + 2 * F], a_rep[al],
                                 start=True, stop=True)
            last.then_inc(wa_done, 1)
            pe.wait_ge(ident_ready, 1)
            pe.wait_ge(x_loaded, 16)
            pe.wait_ge(wcopy_ready, 1)
            for g in range(NG):
                turn_pe(pe, turn_at(0, g), x, g, x_loaded, 16)
                wh_pe(pe, 0, g)
            pe.wait_ge(wsq_ready, 1)
            pe.wait_ge(consts_ready, 1)
            pe.matmul(psum[:, MISC, 256:256 + NL - 1], ones[:, :], w_dst2[:, 1:NL], start=True, stop=True).then_inc(wnorm_done, 1)
            pe.wait_ge(dmax_part, 1)
            pe.wait_ge(lnnorm_ready, 1)
            pe.transpose(psum[0:1, MISC, 0:PART], dmax[:, :], ident[:, :]).then_inc(dmax_turned, 1)
            pe.wait_ge(dmax_one, 1)
            pe.matmul(psum[:, MISC, 384:385], ones[0:1, :], dmax1[:, :], start=True, stop=True).then_inc(dmax_spread, 1)
            for g in range(NG):
                src_pe(pe, 0, g)
            for al in range(NL):
                for g in range(NG):
                    group_sums_pe(pe, al, g)
                if al == 0:
                    group_pe(pe, 0, NG - 1)
                    layer1_pe(pe)


def kernel(x, adj, L0_gnn_W, L0_gnn_a, L1_gnn_w_k, L1_gnn_w_q, L2_gnn_W, L2_gnn_a, L3_gnn_W, L3_gnn_a):
    import numpy as np
    import concourse.bacc as bacc
    from concourse import mybir as _mybir
    from concourse.bass_utils import run_bass_kernel_spmd

    n, f = x.shape
    part, group = 128, 512
    x_rows = np.ascontiguousarray(np.asarray(x).reshape(n // part, part, f).transpose(1, 0, 2)).reshape(part, -1)
    adj_t = np.ascontiguousarray(np.asarray(adj).T.reshape(n // part, part, n // group, group).transpose(2, 1, 0, 3))
    adj_t = adj_t.reshape(n // group, part, -1)
    columns = []
    for w, a in ((L0_gnn_W, L0_gnn_a), (L2_gnn_W, L2_gnn_a), (L3_gnn_W, L3_gnn_a)):
        w, a = np.asarray(w), np.asarray(a)
        columns += [w, w.T, a.reshape(2, f).T]
    weights = np.ascontiguousarray(np.concatenate(columns + [np.asarray(L1_gnn_w_k), np.asarray(L1_gnn_w_q)], axis=1))

    nc = bacc.Bacc("TRN2", target_bir_lowering=False, num_devices=1)
    arrays = {"x_rows": x_rows, "adj_t": adj_t, "weights": weights}
    args = [nc.dram_tensor(name, a.shape, _mybir.dt.from_np(a.dtype), kind="ExternalInput").ap()
            for name, a in arrays.items()]
    out = nc.dram_tensor("out_rows", x_rows.shape, _mybir.dt.float32, kind="ExternalOutput").ap()
    graph_layers(nc, *args, out, slopes=(0.2, 0.2, 0.01))
    got = run_bass_kernel_spmd(nc, [arrays], core_ids=[0]).results[0]["out_rows"]
    return np.ascontiguousarray(np.asarray(got).reshape(part, n // part, f).transpose(1, 0, 2)).reshape(n, f)
```

```python
from contextlib import ExitStack

import concourse.bass as bass
from concourse import mybir

ALU = mybir.AluOpType
ACT = mybir.ActivationFunctionType
F32 = mybir.dt.float32
BF16 = mybir.dt.bfloat16
F16 = mybir.dt.float16
F8 = mybir.dt.float8e4
U8 = mybir.dt.uint8
AX_X = mybir.AxisListType.X


def graph_layers(nc, x_in, adj_in, weights_in, out, slopes):
    PART = 128
    F = 64
    N = x_in.shape[1] // F * PART
    NT = N // PART
    GT = 4
    NG = NT // GT
    GW = GT * PART
    FV = F + 1
    E = 8
    NL = 3
    LW = 2 * F + 2
    STACK = 9 * E
    STACKM = STACK + 3
    SCORE_SCALE = 1.0 / float(E) ** 0.5
    LN_EPS = 1e-5
    LENGTH_BOUND = float(F) ** 0.5 * 1.001
    HALF = F * 2
    VP = 2 * FV
    PART_SCALE = 2.0 ** 12
    LN_PART_SCALE = 12 * 0.6931471805599453
    HIDE = 2.0 ** 40

    with ExitStack() as ctx:
        def sb(name, shape, dt):
            return ctx.enter_context(nc.sbuf_tensor(name, shape, dt))

        def sem(name):
            return ctx.enter_context(nc.semaphore(name))

        adj = sb("adj", [PART, NG, NT, GW], U8)
        prob = sb("prob", [PART, NG, NT, GW], F32)
        x = sb("x", [PART, NT, F], F32)
        y = sb("y", [PART, NT, F], F32)
        val = sb("val", [PART, 2, NT, FV], F32)
        wts = sb("wts", [F, NL * LW + 2 * E], F32)
        a_rep = [prob[0:F, 0, al, 0:PART + 2] for al in range(NL)]
        w_src = sb("w_src", [F, NL, PART], F32)
        w_ext = sb("w_ext", [F, NL, F + 2], F32)
        w_dst2 = sb("w_dst2", [F, NL], F32)
        ident = sb("ident", [PART, PART], F32)
        identb = sb("identb", [PART, PART], BF16)
        hide = sb("hide", [PART, PART], BF16)
        ones = sb("ones", [F, PART], F32)
        cst = sb("cst", [PART, 2], F32)
        powers = sb("powers", [PART, 2, GT], F32)
        xT = sb("xT", [PART, NG, GW], F32)
        sumsT = sb("sumsT", [FV, 2, GW], F32)
        r_row = sb("r_row", [PART, NG, GW], F32)
        stackT = r_row[:, :, :].rearrange("p g i -> p (g i)").bitcast(BF16).rearrange("p (w g i) -> p w g i", w=2, g=NG)
        kT, qT = stackT[0:STACKM, 0], stackT[0:STACKM, 1]
        prob16 = prob[:, :, :, :].bitcast(F16).rearrange("p g t (a i) -> p g t a i", a=2)
        val16 = val[:, :, :, :].bitcast(F16)
        hidden = adj[:, :, :, :].bitcast(F8)
        row_max = xT
        d_col = sb("d_col", [PART, NT], F32)
        b_col = sb("b_col", [PART, 2, NT], F32)
        dmax = sb("dmax", [PART, 1], F32)
        dmax1 = sb("dmax1", [1, 1], F32)
        shift = sb("shift", [PART, NL, 4], F32)
        w_norm = sb("w_norm", [PART, NL], F32)
        w_norm2 = sb("w_norm2", [PART, NL], F32)
        rinv = sb("rinv", [PART, NT], F32)
        h = sb("h", [PART, 2, GT, F], F32)
        e = sb("e", [PART, 2, GT, F], F32)
        stats = sb("stats", [PART, 2, GT, 6], F32)
        mv = sb("mv", [PART, 2, GT, 2], F32)
        v, rstd = (sb(n, [PART, 2, GT], F32) for n in ("v", "rstd"))
        kq = sb("kq", [PART, 3, GT, 2 * E], F32)
        kq_part = sb("kq_part", [PART, 3, GT, 2 * E], BF16)
        k_stack = sb("k_stack", [PART, NT, STACKM], BF16)
        q_stack = y[:, :, :].bitcast(BF16)[:, :, 0:STACKM]
        mx = sb("mx", [PART, 3, NT], F32)

        psum = ctx.enter_context(nc.psum_tensor("psum", [PART, 8, 512], F32))
        TR, SRC, WH, MISC = 4, 5, 6, 7

        def acc(b):
            return psum[:, 2 + b % 2, 0:GT * FV].rearrange("p (t f) -> p t f", f=FV)

        def first_sums(q):
            return psum[:, q // 2, (q % 2) * VP:(q % 2) * VP + HALF + 1]

        def product_sums(k, q):
            return psum[:, k % 2, q * HALF:(q + 1) * HALF]

        def wh(b):
            return psum[:, b, 0:GT * (F + 2)].rearrange("p (t f) -> p t f", f=F + 2)

        def tiles(g):
            return slice(g * GT, (g + 1) * GT)

        SLOT = [0, 1, 0]

        x_loaded = sem("x_loaded")
        w_loaded = sem("w_loaded")
        adj_loaded = [sem(f"adj_loaded{n}") for n in range(NG * 4)]
        stored = sem("stored")
        zeroed = sem("zeroed")
        ident_ready = sem("ident_ready")
        consts_ready = sem("consts_ready")
        arep_ready = sem("arep_ready")
        wa_done = sem("wa_done")
        wcopy_ready = sem("wcopy_ready")
        wsq_ready = sem("wsq_ready")
        wnorm_done = sem("wnorm_done")
        wnorm_ready = sem("wnorm_ready")
        bound_ready = sem("bound_ready")
        dmax_part = sem("dmax_part")
        dmax_turned = sem("dmax_turned")
        dmax_one = sem("dmax_one")
        dmax_spread = sem("dmax_spread")
        dmax_ready = sem("dmax_ready")
        shift_ready = sem("shift_ready")
        tr_done = sem("tr_done")
        xT_ready = sem("xT_ready")
        wh_done = sem("wh_done")
        src_done = sem("src_done")
        d_ready = sem("d_ready")
        relu_ready = sem("relu_ready")
        r_ready = sem("r_ready")
        b_ready = sem("b_ready")
        weight_ready = sem("weight_ready")
        val_ready = sem("val_ready")
        p_ready = sem("p_ready")
        sums_done = sem("sums_done")
        sumsT_ready = sem("sumsT_ready")
        acc_done = sem("acc_done")
        rinv_ready = sem("rinv_ready")
        h_ready = sem("h_ready")
        neg_ready = sem("neg_ready")
        e_ready = sem("e_ready")
        y0_ready = sem("y0_ready")
        y_ready = sem("y_ready")
        stats_ready = sem("stats_ready")
        mv_ready = sem("mv_ready")
        v_ready = sem("v_ready")
        rstd_ready = sem("rstd_ready")
        x_ready = sem("x_ready")
        hn_ready = sem("hn_ready")
        kq_done = sem("kq_done")
        kq_step = sem("kq_step")
        stacks_ready = sem("stacks_ready")
        stackT_done = sem("stackT_done")
        stackT_ready = sem("stackT_ready")
        parts_step = sem("parts_step")
        hidden_ready = sem("hidden_ready")
        adj_back = sem("adj_back")
        max_scores = sem("max_scores")
        rowmax_ready = sem("rowmax_ready")
        rowmax_turned = sem("rowmax_turned")
        mx_ready = sem("mx_ready")
        m_step = sem("m_step")
        mT_done = sem("mT_done")
        mT_ready = sem("mT_ready")
        scores_done = sem("scores_done")
        exp_done = sem("exp_done")
        part_act = sem("part_act")
        part_dve = sem("part_dve")
        pa_ready = sem("pa_ready")
        va_done = sem("va_done")
        va_read = sem("va_read")
        rows_ready = sem("rows_ready")
        va_part = sem("va_part")
        va_ready = sem("va_ready")
        res_ready = sem("res_ready")

        def norm_at(layer, g):
            if layer == 0:
                return 2 * g
            if layer == "h":
                return 2 * g + 1
            return 2 * NG + (layer - 1) * NG + g

        def turn_at(al, g):
            return {0: 0, "h": 1, 1: 2, 2: 3}[al] * NG + g

        LAYER = [0, 2, 3]
        TERM = [1.0, 0.5, 0.0, 1.0 / 6.0]

        block = ctx.enter_context(nc.Block())

        @block.sync
        def _(sp):
            sp.dma_start(x[:, :, :], x_in.rearrange("p (t f) -> p t f", f=F)).then_inc(x_loaded, 16)
            sp.dma_start(wts[:, :], weights_in).then_inc(w_loaded, 16)
            for g in range(NG):
                sp.wait_ge(x_ready, 3 * NG + g + 1)
                sp.dma_start(out[:, g * GT * F:(g + 1) * GT * F],
                             x[:, tiles(g), :].rearrange("p t f -> p (t f)")).then_inc(stored, 16)
            sp.wait_ge(stored, 16 * NG)

        def norm_pool(pool, i, is_h):
            b = i % 2
            pool.wait_ge(mv_ready, i + 1)
            if is_h:
                pool.tensor_scalar(v[:, b, :], mv[:, b, :, 1], float(F), 1e-24, ALU.mult, ALU.max).then_inc(v_ready, 1)
            else:
                pool.tensor_scalar(v[:, b, :], mv[:, b, :, 1], LN_EPS, None, ALU.add).then_inc(v_ready, 1)
            pool.wait_ge(v_ready, i + 1)
            pool.tensor_tensor(rstd[:, b, :], v[:, b, :], powers[:, 0, :], ALU.pow).then_inc(rstd_ready, 1)

        @block.gpsimd
        def _(pool):
            pool.memset(ident[:, :], 0.0).then_inc(zeroed, 1)
            for g in range(NG):
                for c in range(4):
                    pool.dma_start(adj[:, g, 4 * c:4 * c + 4, :],
                                   adj_in[g, :, 4 * c * GW:(4 * c + 4) * GW].rearrange("p (t i) -> p t i", i=GW),
                                   max_dma_last_dim=8192).then_inc(adj_loaded[4 * g + c], 16)
                    if g == 0 and c == 0:
                        pool.wait_ge(zeroed, 1)
                        pool.affine_select(out=ident[:, :], in_=ident[:, :], compare_op=ALU.not_equal, fill=1.0,
                                           base=0, pattern=[[-1, PART]], channel_multiplier=1).then_inc(ident_ready, 1)
            pool.wait_ge(wnorm_ready, 1)
            pool.tensor_tensor(w_norm2[:, 1:NL], w_norm[:, 1:NL], powers[:, 1, 0:NL - 1], ALU.pow).then_inc(wnorm_ready, 1)
            pool.wait_ge(wnorm_ready, 2)
            pool.tensor_scalar(shift[:, 1:NL, 0], w_norm2[:, 1:NL], LENGTH_BOUND, 1e-6, ALU.mult, ALU.add).then_inc(bound_ready, 1)
            for g in range(NG):
                norm_pool(pool, norm_at(0, g), False)
                norm_pool(pool, norm_at("h", g), True)
            for layer in range(1, 4):
                for g in range(NG):
                    norm_pool(pool, norm_at(layer, g), False)

        def turned_act(act, n, g):
            act.wait_ge(tr_done, n + 1)
            act.activation(xT[0:F, g, :], psum[0:F, TR, :], ACT.Copy).then_inc(xT_ready, 1)

        def weights_act(act, al, g):
            k = al * NG + g
            act.wait_ge(shift_ready, 3 * (al + 1))
            act.wait_ge(d_ready, k + 1)
            act.activation(b_col[:, al % 2, tiles(g)], d_col[:, tiles(g)], ACT.Exp, bias=shift[:, al, 2:3],
                           scale=1.0 - slopes[al]).then_inc(b_ready, 1)
            act.activation(val[:, SLOT[al], tiles(g), F], d_col[:, tiles(g)], ACT.Exp, bias=shift[:, al, 3:4],
                           scale=slopes[al]).then_inc(weight_ready, 1)

        def row_act(act, al, g):
            k = al * NG + g
            act.wait_ge(src_done, k + 1)
            act.activation(r_row[:, g, :], psum[:, SRC, :], ACT.Relu, bias=shift[:, al, 1:2],
                           scale=1.0 - slopes[al]).then_inc(relu_ready, 1)
            act.wait_ge(relu_ready, k + 1)
            act.activation(r_row[:, g, :], r_row[:, g, :], ACT.Exp, scale=-1.0).then_inc(r_ready, 1)

        def elu_act(act, al, g):
            k = al * NG + g
            act.wait_ge(h_ready, k + 1)
            act.activation(e[:, k % 2], h[:, k % 2], ACT.Relu, scale=-1.0).then_inc(neg_ready, 1)
            act.wait_ge(neg_ready, k + 1)
            act.activation(e[:, k % 2], e[:, k % 2], ACT.Exp, scale=-1.0).then_inc(e_ready, 1)

        def next_inputs_act(act, al, g):
            turned_act(act, turn_at(al, g), g)
            weights_act(act, al, g)
            row_act(act, al, g)

        def hide_act(act, g):
            act.wait_ge(p_ready, (g + 1) * NT)
            for c in range(4):
                t = slice(4 * c, 4 * c + 4)
                act.activation(hidden[:, g, t, :], adj[:, g, t, :], ACT.Copy, bias=-1.0, saturate=False).then_inc(hidden_ready, 1)

        def show_act(act, g):
            for c in range(4):
                t = slice(4 * c, 4 * c + 4)
                act.activation(adj[:, g, t, :], hidden[:, g, t, :], ACT.Copy, bias=1.0).then_inc(adj_back, 1)

        def sums_act(act, k):
            act.wait_ge(sums_done, k + 1)
            if k > 1:
                act.wait_ge(acc_done, k - 1)
            act.activation(sumsT[:, k % 2, :], psum[0:FV, k % 2, :], ACT.Copy).then_inc(sumsT_ready, 1)

        def layer1_act(act):
            for g in range(NG):
                for which, dst in ((0, kT), (1, qT)):
                    act.wait_ge(stackT_done, 2 * g + which + 1)
                    act.activation(dst[0:STACKM, g, :], turned_stack(which), ACT.Copy).then_inc(stackT_ready, 1)
            for g in range(NG):
                act.wait_ge(mT_done, g + 1)
                act.activation(kT[0:STACKM, g, :], turned_stack(g % 2), ACT.Copy).then_inc(mT_ready, 1)
            for n in range(NG * NT // 2):
                act.wait_ge(scores_done, n + 1)
                act.activation(pair(n), pair(n), ACT.Exp, scale=SCORE_SCALE, bias=cst[:, 1:2]).then_inc(exp_done, 1)
                if part_by_act(n):
                    act.wait_ge(exp_done, n + 1)
                    act.activation(attention(n)[:, :, 0, :], pair(n), ACT.Copy).then_inc(part_act, 1)
            for g in range(NG):
                show_act(act, g)
            for g in range(NG):
                next_inputs_act(act, 1, g)

        def pair(n):
            return psum[:, 2 + 2 * (n % 3):4 + 2 * (n % 3), :]

        def attention(n):
            g, c = divmod(n, NT // 2)
            return prob16[:, g, 2 * c:2 * c + 2]

        def part_by_act(n):
            return n % 4 != 3

        def turned_stack(which):
            return psum[0:STACKM, [SRC, MISC][which], :].bitcast(BF16)[:, 0:GW]

        @block.scalar
        def _(act):
            act.wait_ge(consts_ready, 1)
            for g in range(NG):
                turned_act(act, turn_at(0, g), g)
            for g in range(NG):
                weights_act(act, 0, g)
            for g in range(NG):
                row_act(act, 0, g)
            for al in range(NL):
                for g in range(NG):
                    sums_act(act, al * NG + g)
                    elu_act(act, al, g)
                    if al == 0:
                        turned_act(act, turn_at("h", g), g)
                        hide_act(act, g)
                    if al == 1:
                        next_inputs_act(act, 2, g)
                if al == 0:
                    layer1_act(act)

        def block_dve(dve, al, g, jt):
            if jt == 0:
                dve.wait_ge(r_ready, al * NG + g + 1)
                if al > 0:
                    dve.wait_ge(adj_back, 4 * (g + 1))
                if al == 1:
                    dve.wait_ge(va_done, 3 * NG + g + 1)
                if al == 2:
                    dve.wait_ge(sums_done, NG + g + 1)
            if jt % GT == 0:
                dve.wait_ge(b_ready, al * NG + jt // GT + 1)
                if al == 0:
                    dve.wait_ge(adj_loaded[4 * g + jt // 4], 16)
            dve.scalar_tensor_tensor(out=prob[:, g, jt, :], in0=r_row[:, g, :], scalar=b_col[:, al % 2, jt:jt + 1],
                                     in1=adj[:, g, jt, :], op0=ALU.max, op1=ALU.mult).then_inc(p_ready, 1)

        def elu_dve(dve, al, g, step):
            k = al * NG + g
            b = k % 2
            a = acc(g)
            if step == 0:
                dve.wait_ge(acc_done, k + 1)
                dve.reciprocal(rinv[:, tiles(g)], a[:, :, F]).then_inc(rinv_ready, 1)
            if step == 1:
                dve.wait_ge(rinv_ready, k + 1)
                dve.tensor_tensor(h[:, b], a[:, :, 0:F], rinv[:, tiles(g)].unsqueeze(2).to_broadcast([PART, GT, F]),
                                  ALU.mult).then_inc(h_ready, 1)
            if step == 2:
                dve.wait_ge(h_ready, k + 1)
                dve.scalar_tensor_tensor(out=y[:, tiles(g), :], in0=h[:, b], scalar=0.0, in1=x[:, tiles(g), :],
                                         op0=ALU.max, op1=ALU.add).then_inc(y0_ready, 1)
            if step == 3:
                dve.wait_ge(e_ready, k + 1)
                dve.wait_ge(y0_ready, k + 1)
                dve.scalar_tensor_tensor(out=y[:, tiles(g), :], in0=e[:, b], scalar=-1.0, in1=y[:, tiles(g), :],
                                         op0=ALU.add, op1=ALU.add).then_inc(y_ready, 1)

        def norm_dve(dve, i, g, step, src, dst, given, count, done):
            b = i % 2
            if step == 0:
                dve.wait_ge(given, count)
                for q in range(GT):
                    last = dve.bn_stats(stats[:, b, q, :], src[:, g * GT + q, 0:F])
                last.then_inc(stats_ready, 1)
            if step == 1:
                dve.wait_ge(stats_ready, i + 1)
                for q in range(GT):
                    last = dve.bn_aggr(mv[:, b, q, :], stats[:, b, q, :])
                last.then_inc(mv_ready, 1)
            if step == 2:
                dve.wait_ge(mv_ready, i + 1)
                dve.wait_ge(rstd_ready, i + 1)
                for q in range(GT):
                    last = dve.tensor_scalar(dst[:, g * GT + q, :], src[:, g * GT + q, 0:F], mv[:, b, q, 0:1],
                                             rstd[:, b, q:q + 1], ALU.subtract, ALU.mult)
                last.then_inc(done, 1)

        def layer_norm_dve(dve, layer, g, step):
            norm_dve(dve, norm_at(layer, g), g, step, y, x, y_ready, layer * NG + g + 1, x_ready)

        def d_dve(dve, al, g):
            dve.wait_ge(wh_done, al * NG + g + 1)
            dve.tensor_copy(d_col[:, tiles(g)], wh(g if al == 0 else WH)[:, :, F + 1]).then_inc(d_ready, 1)

        def values_dve(dve, al, g):
            dve.wait_ge(weight_ready, al * NG + g + 1)
            v_g = val[:, SLOT[al], tiles(g), :]
            dve.tensor_tensor(v_g[:, :, 0:F], wh(g if al == 0 else WH)[:, :, 0:F],
                              v_g[:, :, F:F + 1].to_broadcast([PART, GT, F]), ALU.mult).then_inc(val_ready, 1)

        def split_rows_dve(dve, g):
            dve.wait_ge(hn_ready, g + 1)
            rows = y[:, tiles(g), :]
            v16 = val16[:, 1, tiles(g), :]
            dve.tensor_scalar(v16[:, :, 0:F], rows, PART_SCALE, None, ALU.mult).then_inc(parts_step, 1)
            dve.wait_ge(parts_step, 2 * g + 1)
            dve.scalar_tensor_tensor(out=v16[:, :, F:HALF], in0=rows, scalar=PART_SCALE, in1=v16[:, :, 0:F],
                                     op0=ALU.mult, op1=ALU.subtract).then_inc(parts_step, 1)

        def keys_dve(dve, g):
            src = psum[:, WH, 0:GT * 2 * E].rearrange("p (t f) -> p t f", f=2 * E)
            dve.wait_ge(kq_done, g + 1)
            n = 6 * g
            dve.tensor_copy(kq[:, 0], src).then_inc(kq_step, 1)
            for a in range(3):
                n += 1
                dve.wait_ge(kq_step, n)
                dve.tensor_copy(kq_part[:, a], kq[:, a]).then_inc(kq_step, 1)
                if a < 2:
                    n += 1
                    dve.wait_ge(kq_step, n)
                    dve.tensor_tensor(kq[:, a + 1], kq[:, a], kq_part[:, a], ALU.subtract).then_inc(kq_step, 1)
            dve.wait_ge(kq_step, n + 1)
            ks = k_stack[:, tiles(g), 0:STACK].rearrange("p t (a c e) -> p t a c e", a=3, c=3)
            qs = q_stack[:, tiles(g), 0:STACK].rearrange("p t (a c e) -> p t a c e", a=3, c=3)
            for a in range(3):
                dve.tensor_copy(ks[:, :, a, :, :], kq_part[:, a, :, 0:E].unsqueeze(2).to_broadcast([PART, GT, 3, E]))
                last = dve.tensor_copy(qs[:, :, :, a, :],
                                       kq_part[:, a, :, E:2 * E].unsqueeze(2).to_broadcast([PART, GT, 3, E]))
            last = dve.memset(q_stack[:, tiles(g), STACK:STACKM], 1.0)
            last.then_inc(stacks_ready, 1)

        def group_step_dve(dve, al, g, jt):
            if 2 <= jt < 6:
                elu_dve(dve, al, g, jt - 2)
            if jt in (6, 7, 10):
                layer_norm_dve(dve, LAYER[al], g, {6: 0, 7: 1, 10: 2}[jt])
            if al == 0 and jt in (11, 12, 14):
                norm_dve(dve, norm_at("h", g), g, {11: 0, 12: 1, 14: 2}[jt], x, y, x_ready, g + 1, hn_ready)
            if al == 0 and jt == 15:
                split_rows_dve(dve, g)
                keys_dve(dve, g)
            if al == 1 and jt == 11:
                d_dve(dve, 2, g)
            if al == 1 and jt == 12:
                values_dve(dve, 2, g)

        def product_dve(dve, n, g):
            k = n * NG + g
            b = k % 2
            rows = h[:, b]
            v16 = val16[:, n % 2, tiles(g), :]
            dve.wait_ge(va_done, k + 1)
            if n == 0:
                for c in range(2):
                    sums = psum[:, c, 0:2 * VP].rearrange("p (t f) -> p t f", f=VP)
                    dve.reciprocal(rinv[:, g * GT + 2 * c:g * GT + 2 * c + 2], sums[:, :, HALF])
                    last = dve.tensor_reduce(e[:, b, 2 * c:2 * c + 2, :], sums[:, :, 0:HALF].rearrange("p t (a f) -> p t f a", a=2),
                                             AX_X, ALU.add)
            else:
                last = dve.tensor_reduce(e[:, b], psum[:, b, :].rearrange("p (t a f) -> p t f a", t=GT, a=2), AX_X, ALU.add)
            last.then_inc(va_read, 1)
            dve.wait_ge(va_read, k + 1)
            dve.tensor_tensor(rows, e[:, b], rinv[:, tiles(g)].unsqueeze(2).to_broadcast([PART, GT, F]),
                              ALU.mult).then_inc(rows_ready, 1)
            dve.wait_ge(rows_ready, k + 1)
            if n < 3:
                dve.tensor_copy(v16[:, :, 0:F], rows).then_inc(va_part, 1)
                dve.wait_ge(va_part, k + 1)
                dve.tensor_tensor(v16[:, :, F:HALF], rows, v16[:, :, 0:F], ALU.subtract).then_inc(va_ready, 1)
            if n == 2:
                return
            before = x if n == 0 else y
            if n > 0:
                dve.wait_ge(res_ready, (NG if n == 3 else 0) + g + 1)
            dve.scalar_tensor_tensor(out=y[:, tiles(g), :], in0=rows, scalar=TERM[n] / PART_SCALE,
                                     in1=before[:, tiles(g), :], op0=ALU.mult,
                                     op1=ALU.add).then_inc(y_ready if n == 3 else res_ready, 1)

        def layer1_dve(dve):
            for n in range(NT * 2):
                jt, half = divmod(n, 2)
                scores = psum[:, 2 * (n % 4):2 * (n % 4) + 2, :]
                run = row_max[:, 2 * half:2 * half + 2, :]
                dve.wait_ge(max_scores, n + 1)
                if jt == 0:
                    dve.tensor_copy(run, scores).then_inc(rowmax_ready, 1)
                else:
                    dve.wait_ge(rowmax_ready, n - 1)
                    dve.tensor_tensor(run, scores, run, ALU.max).then_inc(rowmax_ready, 1)
            for g in range(NG):
                dve.wait_ge(rowmax_turned, g + 1)
                dve.tensor_reduce(mx[:, 0, tiles(g)], psum[:, g, :].rearrange("p (t j) -> p t j", j=PART), AX_X,
                                  ALU.max, negate=True).then_inc(mx_ready, 1)
            dve.wait_ge(mx_ready, NG)
            for a in range(3):
                if a:
                    dve.wait_ge(m_step, 2 * a)
                dve.tensor_copy(k_stack[:, :, STACK + a], mx[:, a, :]).then_inc(m_step, 1)
                if a < 2:
                    dve.wait_ge(m_step, 2 * a + 1)
                    dve.tensor_tensor(mx[:, a + 1, :], mx[:, a, :], k_stack[:, :, STACK + a],
                                      ALU.subtract).then_inc(m_step, 1)
            for n in range(NG * NT // 2):
                g, c = divmod(n, NT // 2)
                to = attention(n)
                if part_by_act(n):
                    dve.wait_ge(part_act, n + 1 - n // 4)
                else:
                    dve.wait_ge(exp_done, n + 1)
                    dve.tensor_copy(to[:, :, 0, :], pair(n)).then_inc(part_dve, 1)
                    dve.wait_ge(part_dve, n // 4 + 1)
                dve.tensor_tensor(to[:, :, 1, :], pair(n), to[:, :, 0, :], ALU.subtract).then_inc(pa_ready, 1)
                if g > 0 and c == 2:
                    product_dve(dve, 0, g - 1)
            product_dve(dve, 0, NG - 1)
            for n in range(1, 4):
                for g in range(NG):
                    product_dve(dve, n, g)
                    if n == 3:
                        for step in range(3):
                            layer_norm_dve(dve, 1, g, step)
                        d_dve(dve, 1, g)
                        values_dve(dve, 1, g)

        @block.vector
        def _(dve):
            dve.memset(ones[:, :], 1.0)
            dve.memset(cst[:, 0:1], 0.0)
            dve.memset(cst[:, 1:2], LN_PART_SCALE)
            dve.memset(powers[:, 0, :], -0.5)
            dve.memset(powers[:, 1, :], 0.5)
            dve.memset(val16[:, 1, :, HALF:HALF + 1], 1.0)
            dve.memset(k_stack[:, :, STACK:STACKM], 0.0).then_inc(consts_ready, 1)
            dve.wait_ge(w_loaded, 16)
            for al in range(NL):
                o = al * LW + 2 * F
                dve.tensor_copy(w_ext[:, al, 0:F], wts[:, al * LW:al * LW + F])
                dve.tensor_copy(a_rep[al][:, 0:PART], wts[:, o:o + 1].to_broadcast([F, PART]))
                last = dve.tensor_copy(a_rep[al][:, PART:PART + 2], wts[:, o:o + 2])
            last.then_inc(arep_ready, 1)
            dve.wait_ge(wa_done, 1)
            for al in range(NL):
                wa = psum[0:F, 5 + al, 0:PART + 2]
                dve.tensor_copy(w_src[:, al, :], wa[:, 0:PART])
                last = dve.tensor_copy(w_ext[:, al, F:F + 2], wa[:, PART:PART + 2])
            last.then_inc(wcopy_ready, 1)
            dve.wait_ge(wcopy_ready, 1)
            dve.tensor_tensor(w_dst2[:, :], w_ext[:, :, F + 1], w_ext[:, :, F + 1], ALU.mult).then_inc(wsq_ready, 1)
            dve.wait_ge(ident_ready, 1)
            dve.tensor_scalar(hide[:, :], ident[:, :], HIDE, None, ALU.mult)
            dve.tensor_copy(identb[:, :], ident[:, :]).then_inc(consts_ready, 1)
            dve.wait_ge(wnorm_done, 1)
            dve.tensor_copy(w_norm[:, 1:NL], psum[:, MISC, 256:256 + NL - 1]).then_inc(wnorm_ready, 1)
            for g in range(NG):
                d_dve(dve, 0, g)
            dve.wait_ge(d_ready, NG)
            dve.tensor_reduce(dmax[:, :], d_col[:, :], AX_X, ALU.max).then_inc(dmax_part, 1)
            dve.wait_ge(dmax_turned, 1)
            dve.tensor_reduce(dmax1[:, :], psum[0:1, MISC, 0:PART], AX_X, ALU.max).then_inc(dmax_one, 1)
            dve.wait_ge(dmax_spread, 1)
            dve.tensor_copy(shift[:, 0, 0:1], psum[:, MISC, 384:385]).then_inc(dmax_ready, 1)
            dve.wait_ge(dmax_ready, 1)
            for al in range(NL):
                if al == 1:
                    dve.wait_ge(bound_ready, 1)
                c = shift[:, al, 0:1]
                dve.tensor_scalar(shift[:, al, 1:2], c, 1.0 - slopes[al], None, ALU.mult).then_inc(shift_ready, 1)
                dve.tensor_scalar(shift[:, al, 2:3], c, slopes[al] - 1.0, None, ALU.mult).then_inc(shift_ready, 1)
                dve.tensor_scalar(shift[:, al, 3:4], c, -slopes[al], None, ALU.mult).then_inc(shift_ready, 1)
            for g in range(NG):
                values_dve(dve, 0, g)
            for al in range(NL):
                for g in range(NG):
                    for jt in range(NT):
                        block_dve(dve, al, g, jt)
                        if g > 0:
                            group_step_dve(dve, al, g - 1, jt)
                        elif al == 2:
                            group_step_dve(dve, 1, NG - 1, jt)
                if al != 1:
                    for jt in range(NT):
                        group_step_dve(dve, al, NG - 1, jt)
                if al == 0:
                    layer1_dve(dve)

        def turn_pe(pe, n, src, g, given, count):
            pe.wait_ge(given, count)
            if n > 0:
                pe.wait_ge(xT_ready, n)
            for q in range(GT):
                last = pe.transpose(psum[0:F, TR, q * PART:(q + 1) * PART], src[:, g * GT + q, 0:F], ident[:, :])
            last.then_inc(tr_done, 1)

        def wh_pe(pe, al, g):
            k = al * NG + g
            pe.wait_ge(xT_ready, turn_at(al, g) + 1)
            if al > 0 and g > 0:
                pe.wait_ge(val_ready, k)
            for q in range(GT):
                last = pe.matmul(wh(g if al == 0 else WH)[:, q, :], xT[0:F, g, q * PART:(q + 1) * PART], w_ext[:, al, :],
                                 start=(q == 0), stop=(q == GT - 1), skip_group_check=True)
            last.then_inc(wh_done, 1)

        def src_pe(pe, al, g):
            k = al * NG + g
            if k > 0:
                pe.wait_ge(relu_ready, k)
            pe.matmul(psum[:, SRC, :], w_src[:, al, :], xT[0:F, g, :], start=True, stop=True).then_inc(src_done, 1)

        def group_pe(pe, al, g):
            if al == 0:
                turn_pe(pe, turn_at("h", g), y, g, hn_ready, g + 1)
                pe.wait_ge(xT_ready, turn_at("h", g) + 1)
                if g > 0:
                    pe.wait_ge(stacks_ready, g)
                for q in range(GT):
                    last = pe.matmul(psum[:, WH, q * 2 * E:(q + 1) * 2 * E], xT[0:F, g, q * PART:(q + 1) * PART],
                                     wts[:, NL * LW:NL * LW + 2 * E], start=(q == 0), stop=(q == GT - 1),
                                     skip_group_check=True)
                last.then_inc(kq_done, 1)
            if al == 1:
                turn_pe(pe, turn_at(2, g), x, g, x_ready, 2 * NG + g + 1)
                wh_pe(pe, 2, g)
                src_pe(pe, 2, g)

        def turn_back_pe(pe, k):
            pe.wait_ge(sumsT_ready, k + 1)
            if k > 1:
                pe.wait_ge(h_ready, k - 1)
            for q in range(GT):
                last = pe.transpose(acc(k)[:, q, :], sumsT[:, k % 2, q * PART:(q + 1) * PART], ident[0:FV, 0:FV])
            last.then_inc(acc_done, 1)

        def group_sums_pe(pe, al, g):
            k = al * NG + g
            for jt in range(NT):
                pe.wait_ge(p_ready, k * NT + jt + 1)
                if jt % GT == 0:
                    pe.wait_ge(val_ready, al * NG + jt // GT + 1)
                if jt == 0 and al == 0:
                    pe.wait_ge(val_ready, NG)
                if jt == 0 and al == 1:
                    pe.wait_ge(va_read, 4 * NG)
                if jt == 0 and k > 1:
                    pe.wait_ge(sumsT_ready, k - 1)
                last = pe.matmul(psum[0:FV, k % 2, :], val[:, SLOT[al], jt, :], prob[:, g, jt, :],
                                 start=(jt == 0), stop=(jt == NT - 1))
                if jt == 1 and (g > 0 or al == 2):
                    turn_back_pe(pe, k - 1)
                if jt == (14 if al == 0 else 10):
                    if g > 0:
                        group_pe(pe, al, g - 1)
                    elif al == 2:
                        group_pe(pe, 1, NG - 1)
            last.then_inc(sums_done, 1)
            if g == NG - 1 and al != 1:
                turn_back_pe(pe, k)

        def turn_stack_pe(pe, which, g, stack):
            for q in range(GT):
                last = pe.transpose(turned_stack(which)[:, q * PART:(q + 1) * PART], stack[:, g * GT + q, :], identb[:, :])
            return last

        def layer1_pe(pe):
            for g in range(NG):
                pe.wait_ge(stacks_ready, g + 1)
                if g == 0:
                    pe.wait_ge(relu_ready, NG)
                for which, stack in ((0, k_stack), (1, q_stack)):
                    if g > 0:
                        pe.wait_ge(stackT_ready, 2 * g - 1 + which)
                    turn_stack_pe(pe, which, g, stack).then_inc(stackT_done, 1)
            pe.wait_ge(stackT_ready, 2 * NG)
            pe.wait_ge(hidden_ready, 4 * NG)
            for n in range(NT * 2):
                jt, half = divmod(n, 2)
                if n == 0:
                    pe.wait_ge(h_ready, NG)
                if n > 3:
                    pe.wait_ge(rowmax_ready, n - 3)
                for a in range(2):
                    last = scores_pe(pe, psum[:, 2 * (n % 4) + a, :], jt, 2 * half + a, STACK)
                last.then_inc(max_scores, 1)
            pe.wait_ge(rowmax_ready, 2 * NT)
            for g in range(NG):
                for q in range(GT):
                    last = pe.transpose(psum[:, g, q * PART:(q + 1) * PART], row_max[:, g, q * PART:(q + 1) * PART],
                                        ident[:, :])
                last.then_inc(rowmax_turned, 1)
            for g in range(NG):
                pe.wait_ge(m_step, 5)
                if g > 1:
                    pe.wait_ge(mT_ready, g - 1)
                turn_stack_pe(pe, g % 2, g, k_stack).then_inc(mT_done, 1)
            pe.wait_ge(mT_ready, NG)
            pairs = NT // 2
            for n in range(NG * pairs + 2):
                if n < NG * pairs:
                    if n > 2:
                        pe.wait_ge(pa_ready, n - 2)
                    for a in range(2):
                        last = scores_pe(pe, psum[:, 2 + 2 * (n % 3) + a, :], 2 * (n % pairs) + a, n // pairs, STACKM)
                    last.then_inc(scores_done, 1)
                if n >= 2:
                    g, c = divmod(n - 2, pairs)
                    pe.wait_ge(pa_ready, n - 1)
                    if c == 0 and g > 0:
                        pe.wait_ge(va_read, g)
                    for jt in (2 * c, 2 * c + 1):
                        for q in range(GT):
                            for a in range(2):
                                last = pe.matmul(first_sums(q), prob16[:, g, jt, a, q * PART:(q + 1) * PART],
                                                 val16[:, 1, jt, 0:HALF + 1], start=(jt == 0 and q % 2 == 0 and a == 0),
                                                 stop=(jt == NT - 1 and a == 1), skip_group_check=True)
                    if c == pairs - 1:
                        last.then_inc(va_done, 1)
            for n in range(1, 4):
                for g in range(NG):
                    k = n * NG + g
                    pe.wait_ge(va_read, max(k - 1, NG))
                    for q in range(GT):
                        for jt in range(NT):
                            if g == 0 and q == 0 and jt % GT == 0:
                                pe.wait_ge(va_ready, (n - 1) * NG + jt // GT + 1)
                            for a in range(2):
                                last = pe.matmul(product_sums(k, q), prob16[:, g, jt, a, q * PART:(q + 1) * PART],
                                                 val16[:, (n + 1) % 2, jt, 0:HALF], start=(q == 0 and jt == 0 and a == 0),
                                                 stop=(jt == NT - 1 and a == 1), skip_group_check=True)
                    last.then_inc(va_done, 1)
                    if n == 3 and g > 0:
                        inputs_pe(pe, 1, g - 1)
            inputs_pe(pe, 1, NG - 1)

        def scores_pe(pe, to, jt, g, rows):
            pe.matmul(to, hide[:, :], hidden[:, g, jt, :], start=True, stop=False)
            return pe.matmul(to, qT[0:rows, jt // GT, (jt % GT) * PART:(jt % GT + 1) * PART], kT[0:rows, g, :],
                             start=False, stop=True)

        def inputs_pe(pe, al, g):
            turn_pe(pe, turn_at(al, g), x, g, x_ready, NG * (LAYER[al] - 1) + g + 1)
            wh_pe(pe, al, g)
            src_pe(pe, al, g)

        @block.tensor
        def _(pe):
            pe.wait_ge(arep_ready, 1)
            pe.wait_ge(w_loaded, 16)
            for al in range(NL):
                last = pe.matmul(psum[0:F, 5 + al, 0:PART + 2], wts[:, al * LW + F:al * LW + 2 * F], a_rep[al],
                                 start=True, stop=True)
            last.then_inc(wa_done, 1)
            pe.wait_ge(ident_ready, 1)
            pe.wait_ge(x_loaded, 16)
            pe.wait_ge(wcopy_ready, 1)
            for g in range(NG):
                turn_pe(pe, turn_at(0, g), x, g, x_loaded, 16)
                wh_pe(pe, 0, g)
            pe.wait_ge(wsq_ready, 1)
            pe.wait_ge(consts_ready, 1)
            pe.matmul(psum[:, MISC, 256:256 + NL - 1], ones[:, :], w_dst2[:, 1:NL], start=True, stop=True).then_inc(wnorm_done, 1)
            pe.wait_ge(dmax_part, 1)
            pe.wait_ge(wnorm_ready, 1)
            pe.transpose(psum[0:1, MISC, 0:PART], dmax[:, :], ident[:, :]).then_inc(dmax_turned, 1)
            pe.wait_ge(dmax_one, 1)
            pe.matmul(psum[:, MISC, 384:385], ones[0:1, :], dmax1[:, :], start=True, stop=True).then_inc(dmax_spread, 1)
            for g in range(NG):
                src_pe(pe, 0, g)
            for al in range(NL):
                for g in range(NG):
                    group_sums_pe(pe, al, g)
                if al == 0:
                    group_pe(pe, 0, NG - 1)
                    layer1_pe(pe)


def kernel(x, adj, L0_gnn_W, L0_gnn_a, L1_gnn_w_k, L1_gnn_w_q, L2_gnn_W, L2_gnn_a, L3_gnn_W, L3_gnn_a):
    import numpy as np
    import concourse.bacc as bacc
    from concourse import mybir as _mybir
    from concourse.bass_utils import run_bass_kernel_spmd

    n, f = x.shape
    part, group = 128, 512
    x_rows = np.ascontiguousarray(np.asarray(x).reshape(n // part, part, f).transpose(1, 0, 2)).reshape(part, -1)
    adj_t = np.ascontiguousarray(np.asarray(adj).T.reshape(n // part, part, n // group, group).transpose(2, 1, 0, 3))
    adj_t = adj_t.reshape(n // group, part, -1)
    columns = []
    for w, a in ((L0_gnn_W, L0_gnn_a), (L2_gnn_W, L2_gnn_a), (L3_gnn_W, L3_gnn_a)):
        w, a = np.asarray(w), np.asarray(a)
        columns += [w, w.T, a.reshape(2, f).T]
    weights = np.ascontiguousarray(np.concatenate(columns + [np.asarray(L1_gnn_w_k), np.asarray(L1_gnn_w_q)], axis=1))

    nc = bacc.Bacc("TRN2", target_bir_lowering=False, num_devices=1, dynamic_dma_scratch_size=4096)
    arrays = {"x_rows": x_rows, "adj_t": adj_t, "weights": weights}
    args = [nc.dram_tensor(name, a.shape, _mybir.dt.from_np(a.dtype), kind="ExternalInput").ap()
            for name, a in arrays.items()]
    out = nc.dram_tensor("out_rows", x_rows.shape, _mybir.dt.float32, kind="ExternalOutput").ap()
    graph_layers(nc, *args, out, slopes=(0.2, 0.2, 0.01))
    got = run_bass_kernel_spmd(nc, [arrays], core_ids=[0]).results[0]["out_rows"]
    return np.ascontiguousarray(np.asarray(got).reshape(part, n // part, f).transpose(1, 0, 2)).reshape(n, f)
```

```python
from contextlib import ExitStack

import concourse.bass as bass
from concourse import mybir

ALU = mybir.AluOpType
ACT = mybir.ActivationFunctionType
F32 = mybir.dt.float32
BF16 = mybir.dt.bfloat16
F16 = mybir.dt.float16
F8 = mybir.dt.float8e4
U8 = mybir.dt.uint8
AX_X = mybir.AxisListType.X


def graph_layers(nc, x_in, adj_in, weights_in, out, slopes):
    PART = 128
    F = 64
    N = x_in.shape[1] // F * PART
    NT = N // PART
    GT = 4
    NG = NT // GT
    GW = GT * PART
    FV = F + 1
    E = 8
    NL = 3
    LW = 2 * F + 2
    STACK = 9 * E
    STACKM = STACK + 3
    SCORE_SCALE = 1.0 / float(E) ** 0.5
    LN_EPS = 1e-5
    LENGTH_BOUND = float(F) ** 0.5 * 1.001
    BEHIND = 3
    HALF = F * 2
    VP = 2 * FV
    PART_SCALE = 2.0 ** 12
    LN_PART_SCALE = 12 * 0.6931471805599453
    MAX_SCALE = 2.0 ** -6
    ROUNDING = 2.0 ** -11
    RAISED = 60.0
    HIDE = 2.0 ** 21

    with ExitStack() as ctx:
        def sb(name, shape, dt):
            return ctx.enter_context(nc.sbuf_tensor(name, shape, dt))

        def sem(name):
            return ctx.enter_context(nc.semaphore(name))

        adj = sb("adj", [PART, NG, NT, GW], U8)
        prob = sb("prob", [PART, NG, NT, GW], F32)
        x = sb("x", [PART, NT, F], F32)
        y = sb("y", [PART, NT, F], F32)
        val = sb("val", [PART, 2, NT, FV], F32)
        wts = sb("wts", [F, NL * LW + 2 * E], F32)
        a_rep = [prob[0:F, 0, al, 0:PART + 2] for al in range(NL)]
        w_src = sb("w_src", [F, NL, PART], F32)
        w_ext = sb("w_ext", [F, NL, F + 2], F32)
        w_dst2 = sb("w_dst2", [F, NL], F32)
        ident = sb("ident", [PART, PART], F32)
        identb = sb("identb", [PART, PART], BF16)
        identh = sb("identh", [PART, PART], F16)
        hide = sb("hide", [PART, PART], BF16)
        ones = sb("ones", [F, PART], F32)
        cst = sb("cst", [PART, 3], F32)
        powers = sb("powers", [PART, 3, GT], F32)
        xT = sb("xT", [PART, NG, GW], F32)
        sumsT = sb("sumsT", [PART, 2, GW], F32)
        r_row = sb("r_row", [PART, NG, GW], F32)
        stackT = r_row[:, :, :].rearrange("p g i -> p (g i)").bitcast(BF16).rearrange("p (w g i) -> p w g i", w=2, g=NG)
        kT, qT = stackT[0:STACKM, 0], stackT[0:STACKM, 1]
        prob16 = prob[:, :, :, :].bitcast(F16).rearrange("p g t (a i) -> p g t a i", a=2)
        val16 = val[:, :, :, :].bitcast(F16)
        hidden = adj[:, :, :, :].bitcast(F8)
        row_max = xT[:, :, :].rearrange("p g i -> p (g i)").bitcast(F16)[:, 0:N].rearrange("p (g i) -> p g i", g=NG)
        max_stage = sumsT[:, :, :].bitcast(F16).rearrange("p s (a i) -> p s a i", a=2)
        att_stage = [xT[:, 0:2, :], xT[:, 2:4, :], sumsT[:, :, :]]
        d_col = sb("d_col", [PART, NT], F32)
        b_col = sb("b_col", [PART, 2, NT], F32)
        dmax = sb("dmax", [PART, 1], F32)
        dmax1 = sb("dmax1", [1, 1], F32)
        shift = sb("shift", [PART, NL, 4], F32)
        w_norm = sb("w_norm", [PART, NL], F32)
        w_norm2 = sb("w_norm2", [PART, NL], F32)
        rinv = sb("rinv", [PART, NT], F32)
        h = sb("h", [PART, 2, GT, F], F32)
        e = sb("e", [PART, 2, GT, F], F32)
        stats = sb("stats", [PART, 2, GT, 6], F32)
        mv = sb("mv", [PART, 2, GT, 2], F32)
        v, rstd = (sb(n, [PART, 2, 2, GT], F32) for n in ("v", "rstd"))
        h_scaled = sb("h_scaled", [PART, GT, F], F32)
        kq = sb("kq", [PART, 3, GT, 2 * E], F32)
        kq_part = sb("kq_part", [PART, 3, GT, 2 * E], BF16)
        k_stack = sb("k_stack", [PART, NT, STACKM], BF16)
        q_stack = y[:, :, :].bitcast(BF16)[:, :, 0:STACKM]
        mx = sb("mx", [PART, 3, NT], F32)

        psum = ctx.enter_context(nc.psum_tensor("psum", [PART, 8, 512], F32))
        TR, SRC, WH, MISC = 4, 5, 6, 7

        def acc(b):
            return psum[:, 2 + b % 2, 0:GT * FV].rearrange("p (t f) -> p t f", f=FV)

        def first_sums(q):
            return psum[:, q // 2, (q % 2) * VP:(q % 2) * VP + HALF + 1]

        def product_sums(k, q):
            return psum[:, k % 2, q * HALF:(q + 1) * HALF]

        def wh(b):
            return psum[:, b, 0:GT * (F + 2)].rearrange("p (t f) -> p t f", f=F + 2)

        def tiles(g):
            return slice(g * GT, (g + 1) * GT)

        def src_bank(k):
            return psum[:, (SRC, WH, TR, MISC)[k] if k < NG else SRC, :]

        def turn_bank(n):
            return psum[0:F, (TR, SRC, WH, MISC)[n] if n < NG else TR, :]

        SLOT = [0, 1, 0]

        x_loaded = sem("x_loaded")
        w_loaded = sem("w_loaded")
        adj_loaded = [sem(f"adj_loaded{n}") for n in range(NG * 4)]
        stored = sem("stored")
        zeroed = sem("zeroed")
        ident_ready = sem("ident_ready")
        consts_ready = sem("consts_ready")
        arep_ready = sem("arep_ready")
        wa_done = sem("wa_done")
        wcopy_ready = sem("wcopy_ready")
        wsq_ready = sem("wsq_ready")
        wnorm_done = sem("wnorm_done")
        wnorm_ready = sem("wnorm_ready")
        bound_ready = sem("bound_ready")
        dmax_part = sem("dmax_part")
        dmax_turned = sem("dmax_turned")
        dmax_one = sem("dmax_one")
        dmax_spread = sem("dmax_spread")
        dmax_ready = sem("dmax_ready")
        shift_ready = sem("shift_ready")
        tr_done = sem("tr_done")
        xT_ready = sem("xT_ready")
        wh_done = sem("wh_done")
        src_done = sem("src_done")
        d_ready = sem("d_ready")
        relu_ready = sem("relu_ready")
        r_ready = sem("r_ready")
        b_ready = sem("b_ready")
        weight_ready = sem("weight_ready")
        val_ready = sem("val_ready")
        p_ready = sem("p_ready")
        sums_done = sem("sums_done")
        sumsT_ready = sem("sumsT_ready")
        acc_done = sem("acc_done")
        rinv_ready = sem("rinv_ready")
        h_ready = sem("h_ready")
        neg_ready = sem("neg_ready")
        e_ready = sem("e_ready")
        y0_ready = sem("y0_ready")
        y_ready = sem("y_ready")
        stats_ready = sem("stats_ready")
        mv_ready = sem("mv_ready")
        v_ready = sem("v_ready")
        length_ready = sem("length_ready")
        length_power = sem("length_power")
        rstd_ready = sem("rstd_ready")
        x_ready = sem("x_ready")
        hn_ready = sem("hn_ready")
        kq_done = sem("kq_done")
        kq_read = sem("kq_read")
        kq_step = sem("kq_step")
        kq_last_step = sem("kq_last_step")
        stacks_last = sem("stacks_last")
        stacks_ready = sem("stacks_ready")
        stackT_done = sem("stackT_done")
        stackT_ready = sem("stackT_ready")
        parts_step = sem("parts_step")
        hidden_ready = sem("hidden_ready")
        hidden_last = sem("hidden_last")
        adj_back = sem("adj_back")
        max_scores = sem("max_scores")
        max_copied = sem("max_copied")
        rowmax_ready = sem("rowmax_ready")
        rowmax_turned = sem("rowmax_turned")
        mx_ready = sem("mx_ready")
        mx_low = sem("mx_low")
        mx_up = sem("mx_up")
        m_step = sem("m_step")
        mT_done = sem("mT_done")
        mT_ready = sem("mT_ready")
        scores_done = sem("scores_done")
        exp_done = sem("exp_done")
        part_act = sem("part_act")
        part_dve = sem("part_dve")
        pa_ready = sem("pa_ready")
        va_done = sem("va_done")
        va_read = sem("va_read")
        rows_ready = sem("rows_ready")
        va_part = sem("va_part")
        va_ready = sem("va_ready")
        res_ready = sem("res_ready")

        def norm_at(layer, g):
            return layer * NG + g

        def turn_at(al, g):
            return {0: 0, "h": 1, 1: 2, 2: 3}[al] * NG + g

        LAYER = [0, 2, 3]
        TERM = [1.0, 0.5, 0.0, 1.0 / 6.0]

        block = ctx.enter_context(nc.Block())

        @block.sync
        def _(sp):
            sp.dma_start(x[:, :, :], x_in.rearrange("p (t f) -> p t f", f=F)).then_inc(x_loaded, 16)
            sp.dma_start(wts[:, :], weights_in).then_inc(w_loaded, 16)
            for g in range(NG):
                sp.wait_ge(x_ready, 3 * NG + g + 1)
                sp.dma_start(out[:, g * GT * F:(g + 1) * GT * F],
                             x[:, tiles(g), :].rearrange("p t f -> p (t f)")).then_inc(stored, 16)
            sp.wait_ge(stored, 16 * NG)

        def length_norm_pool(pool, g):
            b = norm_at(0, g) % 2
            pool.wait_ge(length_ready, 4 * (g + 1))
            pool.tensor_tensor(rstd[:, b, 0, :], v[:, b, 0, :], powers[:, 0, :], ALU.pow).then_inc(rstd_ready, 1)
            pool.tensor_tensor(rstd[:, b, 1, :], v[:, b, 1, :], powers[:, 0, :], ALU.pow).then_inc(length_power, 1)

        def split_rows(engine, g):
            rows = y[:, tiles(g), :]
            v16 = val16[:, 1, tiles(g), :]
            scaled = h_scaled[:, :, :]
            engine.wait_ge(hn_ready, g + 1)
            engine.tensor_scalar(scaled, rows, PART_SCALE, None, ALU.mult).then_inc(parts_step, 1)
            engine.wait_ge(parts_step, 3 * g + 1)
            engine.tensor_copy(v16[:, :, 0:F], scaled).then_inc(parts_step, 1)
            engine.wait_ge(parts_step, 3 * g + 2)
            engine.tensor_tensor(v16[:, :, F:HALF], scaled, v16[:, :, 0:F], ALU.subtract).then_inc(parts_step, 1)

        def keys(engine, g, step, n, ready):
            for a in range(3):
                if a > 0:
                    engine.wait_ge(step, n)
                engine.tensor_copy(kq_part[:, a], kq[:, a]).then_inc(step, 1)
                n += 1
                if a < 2:
                    engine.wait_ge(step, n)
                    engine.tensor_tensor(kq[:, a + 1], kq[:, a], kq_part[:, a], ALU.subtract).then_inc(step, 1)
                    n += 1
            engine.wait_ge(step, n)
            ks = k_stack[:, tiles(g), 0:STACK].rearrange("p t (a c e) -> p t a c e", a=3, c=3)
            qs = q_stack[:, tiles(g), 0:STACK].rearrange("p t (a c e) -> p t a c e", a=3, c=3)
            for a in range(3):
                engine.tensor_copy(ks[:, :, a, :, :], kq_part[:, a, :, 0:E].unsqueeze(2).to_broadcast([PART, GT, 3, E]))
                engine.tensor_copy(qs[:, :, :, a, :], kq_part[:, a, :, E:2 * E].unsqueeze(2).to_broadcast([PART, GT, 3, E]))
            engine.memset(q_stack[:, tiles(g), STACK:STACKM], 1.0).then_inc(ready, 1)

        @block.gpsimd
        def _(pool):
            pool.memset(ident[:, :], 0.0).then_inc(zeroed, 1)
            for g in range(NG):
                for c in range(4):
                    pool.dma_start(adj[:, g, 4 * c:4 * c + 4, :],
                                   adj_in[g, :, 4 * c * GW:(4 * c + 4) * GW].rearrange("p (t i) -> p t i", i=GW),
                                   max_dma_last_dim=8192).then_inc(adj_loaded[4 * g + c], 16)
                    if g == 0 and c == 0:
                        pool.wait_ge(zeroed, 1)
                        pool.affine_select(out=ident[:, :], in_=ident[:, :], compare_op=ALU.not_equal, fill=1.0,
                                           base=0, pattern=[[-1, PART]], channel_multiplier=1).then_inc(ident_ready, 1)
            pool.wait_ge(wnorm_ready, 1)
            pool.tensor_tensor(w_norm2[:, 1:NL], w_norm[:, 1:NL], powers[:, 1, 0:NL - 1], ALU.pow).then_inc(wnorm_ready, 1)
            pool.wait_ge(wnorm_ready, 2)
            pool.tensor_scalar(shift[:, 1:NL, 0], w_norm2[:, 1:NL], LENGTH_BOUND, 1e-6, ALU.mult,
                               ALU.add).then_inc(bound_ready, 1)
            for g in range(NG):
                length_norm_pool(pool, g)
                split_rows(pool, g)
                if g < NG - 1:
                    pool.wait_ge(kq_read, g + 1)
                    keys(pool, g, kq_step, 5 * g, stacks_ready)
            with pool.Fori(0, 3 * NG // 2) as two:
                for b in range(2):
                    pool.wait_ge(mv_ready, two * 2 + (NG + b + 1))
                    pool.tensor_tensor(v[:, b, 0, :], mv[:, b, :, 1], powers[:, 2, :], ALU.add).then_inc(v_ready, 1)
                    pool.wait_ge(v_ready, two * 2 + (b + 1))
                    pool.tensor_tensor(rstd[:, b, 0, :], v[:, b, 0, :], powers[:, 0, :], ALU.pow).then_inc(rstd_ready, 1)

        def turned_act(act, n, g):
            act.wait_ge(tr_done, n + 1)
            act.activation(xT[0:F, g, :], turn_bank(n), ACT.Copy).then_inc(xT_ready, 1)

        def weights_act(act, al, g):
            k = al * NG + g
            act.wait_ge(shift_ready, 3 * (al + 1))
            act.wait_ge(d_ready, k + 1)
            act.activation(b_col[:, al % 2, tiles(g)], d_col[:, tiles(g)], ACT.Exp, bias=shift[:, al, 2:3],
                           scale=1.0 - slopes[al]).then_inc(b_ready, 1)
            act.activation(val[:, SLOT[al], tiles(g), F], d_col[:, tiles(g)], ACT.Exp, bias=shift[:, al, 3:4],
                           scale=slopes[al]).then_inc(weight_ready, 1)

        def row_act(act, al, g):
            k = al * NG + g
            act.wait_ge(shift_ready, 3 * al + 1)
            act.wait_ge(src_done, k + 1)
            act.activation(r_row[:, g, :], src_bank(k), ACT.Relu, bias=shift[:, al, 1:2],
                           scale=1.0 - slopes[al]).then_inc(relu_ready, 1)
            act.wait_ge(relu_ready, k + 1)
            act.activation(r_row[:, g, :], r_row[:, g, :], ACT.Exp, scale=-1.0,
                           bias=cst[:, 2:3]).then_inc(r_ready, 1)

        def elu_act(act, k, g):
            act.wait_ge(h_ready, k + 1)
            act.activation(e[:, g % 2], h[:, g % 2], ACT.Relu, scale=-1.0).then_inc(neg_ready, 1)
            act.wait_ge(neg_ready, k + 1)
            act.activation(e[:, g % 2], e[:, g % 2], ACT.Exp, scale=-1.0).then_inc(e_ready, 1)

        def next_inputs_act(act, al, g):
            turned_act(act, turn_at(al, g), g)
            weights_act(act, al, g)
            row_act(act, al, g)

        def keys_act(act, g):
            act.wait_ge(kq_done, g + 1)
            if g > 0:
                act.wait_ge(stacks_ready, g)
            act.activation(kq[:, 0], psum[:, WH, 0:GT * 2 * E].rearrange("p (t f) -> p t f", f=2 * E),
                           ACT.Copy).then_inc(kq_read, 1)

        def hide_act(act, g):
            act.wait_ge(p_ready, (g + 1) * NT)
            for c in range(4):
                t = slice(4 * c, 4 * c + 4)
                act.activation(hidden[:, g, t, :], adj[:, g, t, :], ACT.Copy, bias=-1.0,
                               saturate=False).then_inc(hidden_ready, 1)

        def show_act(act, g):
            for c in range(4):
                t = slice(4 * c, 4 * c + 4)
                act.activation(adj[:, g, t, :], hidden[:, g, t, :], ACT.Copy, bias=1.0).then_inc(adj_back, 1)

        def sums_act(act, k, g):
            act.wait_ge(sums_done, k + 1)
            if not isinstance(k, int) or k > 1:
                act.wait_ge(acc_done, k - 1)
            act.activation(sumsT[0:FV, g % 2, :], psum[0:FV, g % 2, :], ACT.Copy).then_inc(sumsT_ready, 1)

        def stack_act(act, g):
            for which, dst in ((0, kT), (1, qT)):
                act.wait_ge(stackT_done, 2 * g + which + 1)
                act.activation(dst[0:STACKM, g, :], turned_stack(which), ACT.Copy).then_inc(stackT_ready, 1)

        def max_act(act, n):
            if not copied_by_act(n):
                return
            jt, half = MAX_PAIRS[n]
            act.wait_ge(max_scores, n + 1)
            if jt == 0:
                to = row_max[:, 2 * half:2 * half + 2, :]
            else:
                to = max_stage[:, copies(n) % 2]
                before = nth_copied(copies(n) - 2) if copies(n) > 2 else 0
                if MAX_PAIRS[before][0] > 0:
                    act.wait_ge(rowmax_ready, maxima(before))
            act.activation(to, max_pair(n), ACT.Copy, scale=MAX_SCALE).then_inc(max_copied, 1)

        def layer1_act(act):
            for g in range(2):
                stack_act(act, g)
            for n in range(3):
                max_act(act, n)
            turned_act(act, turn_at("h", NG - 1), NG - 1)
            keys_act(act, NG - 1)
            stack_act(act, 2)
            for n in range(4, EARLY):
                max_act(act, n)
            stack_act(act, NG - 1)
            for n in range(EARLY, 2 * NT):
                max_act(act, n)
            for n in range(NG * NT // 2):
                if n in (0, 2):
                    for g in (n, n + 1):
                        act.wait_ge(mT_done, g + 1)
                        act.activation(kT[0:STACKM, g, :], turned_stack(2 + g), ACT.Copy).then_inc(mT_ready, 1)
                act.wait_ge(scores_done, n + 1)
                if n > 2:
                    act.wait_ge(pa_ready, n - 2)
                act.activation(att_stage[n % 3], pair(n), ACT.Exp, scale=SCORE_SCALE, bias=cst[:, 1:2]).then_inc(exp_done, 1)
                if part_by_act(n):
                    act.wait_ge(exp_done, n + 1)
                    act.activation(attention(n)[:, :, 0, :], att_stage[n % 3], ACT.Copy).then_inc(part_act, 1)
            for g in range(NG):
                show_act(act, g)
            for g in range(NG):
                next_inputs_act(act, 1, g)

        EARLY = 2 * GT
        MAX_PAIRS = ([(jt, 0) for jt in range(EARLY)] + [(jt, 1) for jt in range(EARLY)]
                     + [(jt, half) for jt in range(EARLY, NT) for half in range(2)])

        def max_banks(n):
            return 2 * (n % 2) if n < EARLY else 2 * (n % 4)

        def max_pair(n):
            return psum[:, max_banks(n):max_banks(n) + 2, :]

        def last_in_banks(n):
            return max((m for m in range(n) if max_banks(m) == max_banks(n)), default=None)

        def last_of_half(n):
            return max(m for m in range(n) if MAX_PAIRS[m][1] == MAX_PAIRS[n][1])

        def maxima(n):
            return n if n < EARLY else n - 1

        def wait_max_read(engine, n):
            if copied_by_act(n):
                engine.wait_ge(max_copied, copies(n))
            else:
                engine.wait_ge(rowmax_ready, maxima(n))

        def copied_by_act(n):
            return n % 4 != 3

        def copies(n):
            return n + 1 - (n + 1) // 4

        def nth_copied(i):
            return i - 1 + (i - 1) // 3

        def pair(n):
            return psum[:, 2 + 2 * (n % 3):4 + 2 * (n % 3), :]

        def attention(n):
            g, c = divmod(n, NT // 2)
            return prob16[:, g, 2 * c:2 * c + 2]

        def part_by_act(n):
            return n % 2 == 1

        def turned_max(g):
            return psum[:, (2, 3, 0, 1)[g], 0:GW // 2].bitcast(F16)

        def turned_stack(which):
            return psum[0:STACKM, (SRC, MISC, 6, 7, 0, 1)[which], :].bitcast(BF16)[:, 0:GW]

        @block.scalar
        def _(act):
            act.wait_ge(consts_ready, 1)
            for g in range(NG):
                turned_act(act, turn_at(0, g), g)
            row_act(act, 0, 0)
            for g in range(NG):
                weights_act(act, 0, g)
            for g in range(1, NG):
                row_act(act, 0, g)
            for g in range(NG):
                if g > 0:
                    turned_act(act, turn_at("h", g - 1), g - 1)
                sums_act(act, g, g)
                if g > 0:
                    keys_act(act, g - 1)
                elu_act(act, g, g)
                if g < NG - 1:
                    hide_act(act, g)
            layer1_act(act)
            for g in range(NG):
                sums_act(act, NG + g, g)
                elu_act(act, NG + g, g)
                next_inputs_act(act, 2, g)
            with act.Fori(0, NG // 2) as two:
                for b in range(2):
                    sums_act(act, two * 2 + (2 * NG + b), b)
                    elu_act(act, two * 2 + (2 * NG + b), b)

        def block_dve(dve, al, g, jt):
            if jt == 0:
                dve.wait_ge(r_ready, al * NG + g + 1)
                if al > 0:
                    dve.wait_ge(adj_back, 4 * (g + 1))
                if al == 1:
                    dve.wait_ge(va_done, 3 * NG + g + 1)
                if al == 2:
                    dve.wait_ge(sums_done, NG + g + 1)
            if jt % GT == 0:
                dve.wait_ge(b_ready, al * NG + jt // GT + 1)
                if al == 0:
                    dve.wait_ge(adj_loaded[4 * g + jt // 4], 16)
            dve.scalar_tensor_tensor(out=prob[:, g, jt, :], in0=r_row[:, g, :], scalar=b_col[:, al % 2, jt:jt + 1],
                                     in1=adj[:, g, jt, :], op0=ALU.max, op1=ALU.mult).then_inc(p_ready, 1)

        def elu_dve(dve, al, g, step):
            k = al * NG + g
            b = k % 2
            a = acc(g)
            if step == 0:
                dve.wait_ge(acc_done, k + 1)
                dve.reciprocal(rinv[:, tiles(g)], a[:, :, F]).then_inc(rinv_ready, 1)
            if step == 1:
                dve.wait_ge(rinv_ready, k + 1)
                dve.tensor_tensor(h[:, b], a[:, :, 0:F], rinv[:, tiles(g)].unsqueeze(2).to_broadcast([PART, GT, F]),
                                  ALU.mult).then_inc(h_ready, 1)
            if step == 2:
                dve.wait_ge(h_ready, k + 1)
                dve.scalar_tensor_tensor(out=y[:, tiles(g), :], in0=h[:, b], scalar=0.0, in1=x[:, tiles(g), :],
                                         op0=ALU.max, op1=ALU.add).then_inc(y0_ready, 1)
            if step == 3:
                dve.wait_ge(e_ready, k + 1)
                dve.wait_ge(y0_ready, k + 1)
                dve.scalar_tensor_tensor(out=y[:, tiles(g), :], in0=e[:, b], scalar=-1.0, in1=y[:, tiles(g), :],
                                         op0=ALU.add, op1=ALU.add).then_inc(y_ready, 1)

        def layer_norm_dve(dve, layer, g, step):
            i = norm_at(layer, g)
            b = i % 2
            if step == 0:
                dve.wait_ge(y_ready, i + 1)
                for q in range(GT):
                    last = dve.bn_stats(stats[:, b, q, :], y[:, g * GT + q, :])
                last.then_inc(stats_ready, 1)
            if step == 1:
                dve.wait_ge(stats_ready, i + 1)
                for q in range(GT):
                    last = dve.bn_aggr(mv[:, b, q, :], stats[:, b, q, :])
                last.then_inc(mv_ready, 1)
                if layer == 0:
                    variance = mv[:, b, :, 1]
                    dve.wait_ge(mv_ready, i + 1)
                    dve.tensor_scalar(v[:, b, 0, :], variance, LN_EPS, None, ALU.add).then_inc(length_ready, 1)
                    dve.wait_ge(length_ready, 4 * g + 1)
                    dve.reciprocal(v[:, b, 1, :], v[:, b, 0, :]).then_inc(length_ready, 1)
                    dve.wait_ge(length_ready, 4 * g + 2)
                    dve.scalar_tensor_tensor(out=v[:, b, 1, :], in0=variance, scalar=float(F), in1=v[:, b, 1, :],
                                             op0=ALU.mult, op1=ALU.mult).then_inc(length_ready, 1)
                    dve.wait_ge(length_ready, 4 * g + 3)
                    dve.tensor_scalar(v[:, b, 1, :], v[:, b, 1, :], 1e-24, None, ALU.max).then_inc(length_ready, 1)
            if step == 2:
                dve.wait_ge(mv_ready, i + 1)
                dve.wait_ge(rstd_ready, i + 1)
                for q in range(GT):
                    last = dve.tensor_scalar(x[:, g * GT + q, :], y[:, g * GT + q, :], mv[:, b, q, 0:1],
                                             rstd[:, b, 0, q:q + 1], ALU.subtract, ALU.mult)
                last.then_inc(x_ready, 1)

        def unit_rows_dve(dve, g):
            dve.wait_ge(x_ready, g + 1)
            dve.wait_ge(length_power, g + 1)
            dve.tensor_tensor(y[:, tiles(g), :], x[:, tiles(g), :],
                              rstd[:, norm_at(0, g) % 2, 1, :].unsqueeze(2).to_broadcast([PART, GT, F]),
                              ALU.mult).then_inc(hn_ready, 1)

        def shift_dve(dve, al):
            c = shift[:, al, 0:1]
            for n, (factor, raised) in enumerate(((1.0 - slopes[al], 0.0), (slopes[al] - 1.0, RAISED), (-slopes[al], 0.0))):
                dve.tensor_scalar(shift[:, al, 1 + n:2 + n], c, factor, raised, ALU.mult, ALU.add).then_inc(shift_ready, 1)

        def d_dve(dve, al, g):
            dve.wait_ge(wh_done, al * NG + g + 1)
            dve.tensor_copy(d_col[:, tiles(g)], wh(g if al == 0 else WH)[:, :, F + 1]).then_inc(d_ready, 1)

        def values_dve(dve, al, g):
            dve.wait_ge(weight_ready, al * NG + g + 1)
            v_g = val[:, SLOT[al], tiles(g), :]
            dve.tensor_tensor(v_g[:, :, 0:F], wh(g if al == 0 else WH)[:, :, 0:F],
                              v_g[:, :, F:F + 1].to_broadcast([PART, GT, F]), ALU.mult).then_inc(val_ready, 1)

        BESIDE = {6: "elu0", 7: "elu1", 8: "elu2", 9: "elu3", 10: "norm0", 11: "norm1", 13: "norm2",
                  14: "unit", 19: "d", 20: "values"}
        BESIDE_EARLY = {4: "elu0", 5: "elu1", 6: "elu2", 7: "elu3", 8: "norm0", 9: "norm1", 10: "norm2",
                        11: "d, values"}
        BESIDE_LAST = {1: "elu0", 2: "elu1", 3: "hide0, elu2", 4: "elu3", 5: "norm0", 7: "norm1, hide1",
                       9: "norm2", 10: "unit, max1, max2", 11: "hide2, max3", 12: "keys",
                       13: "max4, max5, hide3, max6, max7"}

        def group_step_dve(dve, al, g, at):
            schedule = BESIDE if g < NG - 1 or al == 2 else BESIDE_LAST if al == 0 else BESIDE_EARLY
            for what in schedule.get(at, "").split(", "):
                step = int(what[-1]) if what[-1:].isdigit() else 0
                if what.startswith("elu"):
                    elu_dve(dve, al, g, step)
                if what.startswith("norm"):
                    layer_norm_dve(dve, LAYER[al], g, step)
                if what.startswith("hide"):
                    hide_dve(dve, step)
                if what.startswith("max"):
                    max_dve(dve, step)
                if al == 0 and what == "unit":
                    unit_rows_dve(dve, g)
                if al == 0 and what == "keys":
                    dve.wait_ge(kq_read, NG)
                    dve.wait_ge(stacks_ready, NG - 1)
                    dve.wait_ge(parts_step, 3 * (NG - 1) + 1)
                    keys(dve, g, kq_last_step, 0, stacks_last)
                if al == 1 and what == "d":
                    d_dve(dve, 2, g)
                if al == 1 and what == "values":
                    values_dve(dve, 2, g)

        def hide_dve(dve, c):
            t = slice(4 * c, 4 * c + 4)
            dve.tensor_scalar(hidden[:, NG - 1, t, :], adj[:, NG - 1, t, :], -1.0, None, ALU.add,
                              saturate=False).then_inc(hidden_last, 1)

        def blocks_dve(dve, first, groups):
            for n in range(first, (len(groups) + 2) * NT):
                if n < len(groups) * NT:
                    block_dve(dve, *groups[n // NT], n % NT)
                for k, (al, g) in enumerate(groups):
                    if n >= (k + 1) * NT:
                        group_step_dve(dve, al, g, n - (k + 1) * NT)

        def product_dve(dve, n, g):
            product_sums_dve(dve, n, g)
            product_rows_dve(dve, n, g)

        def product_sums_dve(dve, n, g):
            k = n * NG + g
            b = k % 2
            dve.wait_ge(va_done, k + 1)
            if n == 0:
                for c in range(2):
                    sums = psum[:, c, 0:2 * VP].rearrange("p (t f) -> p t f", f=VP)
                    dve.reciprocal(rinv[:, g * GT + 2 * c:g * GT + 2 * c + 2], sums[:, :, HALF])
                    parts = sums[:, :, 0:HALF].rearrange("p t (a f) -> p t f a", a=2)
                    last = dve.tensor_reduce(e[:, b, 2 * c:2 * c + 2, :], parts, AX_X, ALU.add)
            else:
                last = dve.tensor_reduce(e[:, b], psum[:, b, :].rearrange("p (t a f) -> p t f a", t=GT, a=2), AX_X, ALU.add)
            last.then_inc(va_read, 1)

        def product_rows_dve(dve, n, g):
            k = n * NG + g
            b = k % 2
            rows = h[:, b]
            v16 = val16[:, n % 2, tiles(g), :]
            dve.wait_ge(va_read, k + 1)
            dve.tensor_tensor(rows, e[:, b], rinv[:, tiles(g)].unsqueeze(2).to_broadcast([PART, GT, F]),
                              ALU.mult).then_inc(rows_ready, 1)
            dve.wait_ge(rows_ready, k + 1)
            if n < 3:
                dve.tensor_copy(v16[:, :, 0:F], rows).then_inc(va_part, 1)
                dve.wait_ge(va_part, k + 1)
                dve.tensor_tensor(v16[:, :, F:HALF], rows, v16[:, :, 0:F], ALU.subtract).then_inc(va_ready, 1)
            if n == 2:
                return
            before = x if n == 0 else y
            if n > 0:
                dve.wait_ge(res_ready, (NG if n == 3 else 0) + g + 1)
            dve.scalar_tensor_tensor(out=y[:, tiles(g), :], in0=rows, scalar=TERM[n] / PART_SCALE,
                                     in1=before[:, tiles(g), :], op0=ALU.mult,
                                     op1=ALU.add).then_inc(y_ready if n == 3 else res_ready, 1)

        def max_dve(dve, n):
            jt, half = MAX_PAIRS[n]
            if jt == 0:
                return
            run = row_max[:, 2 * half:2 * half + 2, :]
            if copied_by_act(n):
                dve.wait_ge(max_copied, copies(n))
                scores, scale = max_stage[:, copies(n) % 2], 1.0
            else:
                dve.wait_ge(max_scores, n + 1)
                scores, scale = max_pair(n), MAX_SCALE
            before = last_of_half(n)
            if jt == 1:
                dve.wait_ge(max_copied, copies(before))
            else:
                dve.wait_ge(rowmax_ready, maxima(before))
            if scale == 1.0:
                dve.tensor_tensor(run, scores, run, ALU.max).then_inc(rowmax_ready, 1)
            else:
                dve.scalar_tensor_tensor(out=run, in0=scores, scalar=scale, in1=run, op0=ALU.mult,
                                         op1=ALU.max).then_inc(rowmax_ready, 1)

        def row_max_dve(dve, half):
            for g in (2 * half, 2 * half + 1):
                dve.wait_ge(rowmax_turned, g + 1)
                dve.tensor_reduce(mx[:, 0, tiles(g)], turned_max(g).rearrange("p (t j) -> p t j", j=PART), AX_X, ALU.max,
                                  negate=True).then_inc(mx_ready, 1)
            rows = slice(2 * half * GT, 2 * (half + 1) * GT)
            dve.wait_ge(mx_ready, 2 * (half + 1))
            dve.tensor_scalar(mx[:, 1, rows], mx[:, 0, rows], (1.0 - ROUNDING) / MAX_SCALE, None,
                              ALU.mult).then_inc(mx_low, 1)
            dve.wait_ge(mx_low, half + 1)
            dve.scalar_tensor_tensor(out=mx[:, 0, rows], in0=mx[:, 0, rows], scalar=(1.0 + ROUNDING) / MAX_SCALE,
                                     in1=mx[:, 1, rows], op0=ALU.mult, op1=ALU.min).then_inc(mx_up, 1)
            dve.wait_ge(mx_up, half + 1)
            for a in range(3):
                if a:
                    dve.wait_ge(m_step, 5 * half + 2 * a)
                dve.tensor_copy(k_stack[:, rows, STACK + a], mx[:, a, rows]).then_inc(m_step, 1)
                if a < 2:
                    dve.wait_ge(m_step, 5 * half + 2 * a + 1)
                    dve.tensor_tensor(mx[:, a + 1, rows], mx[:, a, rows], k_stack[:, rows, STACK + a],
                                      ALU.subtract).then_inc(m_step, 1)

        def layer1_dve(dve):
            for n in range(EARLY, 2 * NT):
                max_dve(dve, n)
            for half in range(2):
                row_max_dve(dve, half)
            for n in range(NG * NT // 2):
                g, c = divmod(n, NT // 2)
                to = attention(n)
                if g > 0 and c == BEHIND - 1:
                    product_sums_dve(dve, 0, g - 1)
                if part_by_act(n):
                    dve.wait_ge(part_act, n // 2 + 1)
                else:
                    dve.wait_ge(exp_done, n + 1)
                    dve.tensor_copy(to[:, :, 0, :], att_stage[n % 3]).then_inc(part_dve, 1)
                    dve.wait_ge(part_dve, n // 2 + 1)
                dve.tensor_tensor(to[:, :, 1, :], att_stage[n % 3], to[:, :, 0, :], ALU.subtract).then_inc(pa_ready, 1)
                if g > 0 and c == BEHIND + 1:
                    product_rows_dve(dve, 0, g - 1)
            product_dve(dve, 0, NG - 1)
            for n in range(1, 4):
                for g in range(NG):
                    product_dve(dve, n, g)
                    if n == 3:
                        early = range((g - 1) * GT, g * GT) if g > 0 else ()
                        layer_norm_dve(dve, 1, g, 0)
                        layer_norm_dve(dve, 1, g, 1)
                        for jt in early[:2]:
                            block_dve(dve, 1, 0, jt)
                        layer_norm_dve(dve, 1, g, 2)
                        for jt in early[2:]:
                            block_dve(dve, 1, 0, jt)
                        d_dve(dve, 1, g)
                        values_dve(dve, 1, g)
            for jt in range((NG - 1) * GT, NT):
                block_dve(dve, 1, 0, jt)

        @block.vector
        def _(dve):
            dve.memset(ones[:, :], 1.0)
            dve.memset(cst[:, 0:1], 0.0)
            dve.memset(cst[:, 1:2], LN_PART_SCALE)
            dve.memset(cst[:, 2:3], RAISED)
            dve.memset(powers[:, 0, :], -0.5)
            dve.memset(powers[:, 1, :], 0.5)
            dve.memset(powers[:, 2, :], LN_EPS)
            dve.memset(val16[:, 1, :, HALF:HALF + 1], 1.0)
            dve.memset(k_stack[:, :, STACK:STACKM], 0.0).then_inc(consts_ready, 1)
            dve.wait_ge(w_loaded, 16)
            for al in range(NL):
                o = al * LW + 2 * F
                dve.tensor_copy(w_ext[:, al, 0:F], wts[:, al * LW:al * LW + F])
                dve.tensor_copy(a_rep[al][:, 0:PART], wts[:, o:o + 1].to_broadcast([F, PART]))
                last = dve.tensor_copy(a_rep[al][:, PART:PART + 2], wts[:, o:o + 2])
            last.then_inc(arep_ready, 1)
            dve.wait_ge(wa_done, 1)
            for al in range(NL):
                dve.tensor_copy(w_ext[:, al, F:F + 2], psum[0:F, al, PART:PART + 2]).then_inc(wcopy_ready, 1)
            for al in range(NL):
                dve.tensor_copy(w_src[:, al, :], psum[0:F, al, 0:PART]).then_inc(wcopy_ready, 1)
            dve.wait_ge(wcopy_ready, 2 * NL)
            dve.tensor_tensor(w_dst2[:, :], w_ext[:, :, F + 1], w_ext[:, :, F + 1], ALU.mult).then_inc(wsq_ready, 1)
            dve.wait_ge(ident_ready, 1)
            dve.tensor_scalar(hide[:, :], ident[:, :], HIDE, None, ALU.mult)
            dve.tensor_copy(identh[:, :], ident[:, :])
            dve.tensor_copy(identb[:, :], ident[:, :]).then_inc(consts_ready, 1)
            for g in range(NG):
                d_dve(dve, 0, g)
            dve.wait_ge(d_ready, NG)
            dve.tensor_reduce(dmax[:, :], d_col[:, :], AX_X, ALU.max).then_inc(dmax_part, 1)
            dve.wait_ge(wnorm_done, 1)
            dve.tensor_copy(w_norm[:, 1:NL], psum[:, MISC, 256:256 + NL - 1]).then_inc(wnorm_ready, 1)
            dve.wait_ge(dmax_turned, 1)
            dve.tensor_reduce(dmax1[:, :], psum[0:1, MISC, 0:PART], AX_X, ALU.max).then_inc(dmax_one, 1)
            dve.wait_ge(dmax_spread, 1)
            dve.tensor_copy(shift[:, 0, 0:1], psum[:, MISC, 384:385]).then_inc(dmax_ready, 1)
            dve.wait_ge(dmax_ready, 1)
            shift_dve(dve, 0)
            for g in range(NG):
                values_dve(dve, 0, g)
            dve.wait_ge(bound_ready, 1)
            for al in range(1, NL):
                shift_dve(dve, al)
            blocks_dve(dve, 0, [(0, g) for g in range(NG)])
            layer1_dve(dve)
            blocks_dve(dve, NT, [(al, g) for al in (1, 2) for g in range(NG)])

        def turn_pe(pe, n, src, g, given, count):
            pe.wait_ge(given, count)
            if n >= NG:
                pe.wait_ge(xT_ready, n)
            if n == NG:
                pe.wait_ge(relu_ready, NG)
            for q in range(GT):
                last = pe.transpose(turn_bank(n)[:, q * PART:(q + 1) * PART], src[:, g * GT + q, 0:F], ident[:, :])
            last.then_inc(tr_done, 1)

        def wh_pe(pe, al, g):
            k = al * NG + g
            pe.wait_ge(xT_ready, turn_at(al, g) + 1)
            if al > 0 and g > 0:
                pe.wait_ge(val_ready, k)
            for q in range(GT):
                last = pe.matmul(wh(g if al == 0 else WH)[:, q, :], xT[0:F, g, q * PART:(q + 1) * PART], w_ext[:, al, :],
                                 start=(q == 0), stop=(q == GT - 1), skip_group_check=True)
            last.then_inc(wh_done, 1)

        def src_pe(pe, al, g):
            k = al * NG + g
            if al == 0:
                pe.wait_ge(xT_ready, NG)
            else:
                pe.wait_ge(relu_ready, k)
            pe.matmul(src_bank(k), w_src[:, al, :], xT[0:F, g, :], start=True, stop=True).then_inc(src_done, 1)

        def keys_pe(pe, g):
            pe.wait_ge(xT_ready, turn_at("h", g) + 1)
            if g > 0:
                pe.wait_ge(kq_read, g)
            for q in range(GT):
                last = pe.matmul(psum[:, WH, q * 2 * E:(q + 1) * 2 * E], xT[0:F, g, q * PART:(q + 1) * PART],
                                 wts[:, NL * LW:NL * LW + 2 * E], start=(q == 0), stop=(q == GT - 1),
                                 skip_group_check=True)
            last.then_inc(kq_done, 1)

        def turn_rows_pe(pe, al, g):
            turn_pe(pe, turn_at(al, g), x, g, x_ready, NG * LAYER[al - 1] + g + 1 if al == 2 else NG + g + 1)

        def inputs_pe(pe, al, g):
            wh_pe(pe, al, g)
            src_pe(pe, al, g)

        def turn_back_pe(pe, k):
            pe.wait_ge(sumsT_ready, k + 1)
            if k > 1:
                pe.wait_ge(h_ready, k - 1)
            for q in range(GT):
                last = pe.transpose(acc(k)[:, q, :], sumsT[0:FV, k % 2, q * PART:(q + 1) * PART], ident[0:FV, 0:FV])
            last.then_inc(acc_done, 1)

        def group_sums_pe(pe, al, g):
            k = al * NG + g
            for jt in range(NT):
                pe.wait_ge(p_ready, k * NT + jt + 1)
                if jt % GT == 0:
                    pe.wait_ge(val_ready, al * NG + jt // GT + 1)
                if jt == 0 and al == 0:
                    pe.wait_ge(val_ready, NG)
                if jt == 0 and al == 1 and g < 2:
                    pe.wait_ge(va_read, 4 * NG - 1 + g)
                if jt == 0 and k > 1:
                    pe.wait_ge(sumsT_ready, k - 1)
                last = pe.matmul(psum[0:FV, k % 2, :], val[:, SLOT[al], jt, :], prob[:, g, jt, :],
                                 start=(jt == 0), stop=(jt == NT - 1))
                if jt == NT - 1:
                    last.then_inc(sums_done, 1)
                if jt == 1 and (g > 0 or al == 2):
                    turn_back_pe(pe, k - 1)
                if al == 0 and g > 0 and jt == 15:
                    turn_pe(pe, turn_at("h", g - 1), y, g - 1, hn_ready, g)
                if al == 0 and g > 1 and jt == 1:
                    keys_pe(pe, g - 2)
                if al == 1 and g == 0 and jt == 7:
                    turn_rows_pe(pe, 1, NG - 1)
                if al == 1 and g == 0 and jt == 9:
                    inputs_pe(pe, 1, NG - 1)
                if al == 1 and g > 0 and jt == 13:
                    turn_rows_pe(pe, 2, g - 1)
                if al == 1 and g > 0 and jt == 15:
                    inputs_pe(pe, 2, g - 1)
                if al == 2 and g == 0 and jt == 9:
                    turn_rows_pe(pe, 2, NG - 1)
                if al == 2 and g == 0 and jt == 10:
                    inputs_pe(pe, 2, NG - 1)
            if g == NG - 1 and al != 1:
                turn_back_pe(pe, k)
            if g == NG - 1 and al == 0:
                keys_pe(pe, NG - 2)

        def turn_stack_pe(pe, which, g, stack):
            for q in range(GT):
                last = pe.transpose(turned_stack(which)[:, q * PART:(q + 1) * PART], stack[:, g * GT + q, :], identb[:, :])
            return last

        def stack_pe(pe, g):
            if g == NG - 1:
                pe.wait_ge(stacks_last, 1)
            else:
                pe.wait_ge(stacks_ready, g + 1)
            for which, stack in ((0, k_stack), (1, q_stack)):
                if g > 0:
                    pe.wait_ge(stackT_ready, 2 * g - 1 + which)
                turn_stack_pe(pe, which, g, stack).then_inc(stackT_done, 1)

        def max_pe(pe, n):
            jt, half = MAX_PAIRS[n]
            if half == 1 and jt % GT == 0:
                pe.wait_ge(hidden_last, jt // GT + 1)
            if last_in_banks(n) is not None:
                wait_max_read(pe, last_in_banks(n))
            for a in range(2):
                last = scores_pe(pe, max_pair(n)[:, a, :], jt, 2 * half + a, STACK)
            last.then_inc(max_scores, 1)

        def pair_scores_pe(pe, n):
            g, c = divmod(n, NT // 2)
            if c == 0:
                pe.wait_ge(mT_ready, g + 1)
            if n == 2:
                pe.wait_ge(mT_ready, 2)
            if n > 2:
                pe.wait_ge(exp_done, n - 2)
            for a in range(2):
                last = scores_pe(pe, pair(n)[:, a, :], 2 * c + a, g, STACKM)
            last.then_inc(scores_done, 1)

        def first_product_pe(pe, n):
            g, c = divmod(n, NT // 2)
            if n == 0:
                pe.wait_ge(parts_step, 3 * NG)
                pe.wait_ge(mT_ready, NG)
            pe.wait_ge(pa_ready, n + 1)
            if c == 0 and g > 0:
                pe.wait_ge(va_read, g)
            for jt in (2 * c, 2 * c + 1):
                for q in range(GT):
                    for a in range(2):
                        last = pe.matmul(first_sums(q), prob16[:, g, jt, a, q * PART:(q + 1) * PART],
                                         val16[:, 1, jt, 0:HALF + 1], start=(jt == 0 and q % 2 == 0 and a == 0),
                                         stop=(jt == NT - 1 and a == 1), skip_group_check=True)
            if c == NT // 2 - 1:
                last.then_inc(va_done, 1)

        def layer1_pe(pe):
            pe.wait_ge(relu_ready, NG)
            for g in range(2):
                stack_pe(pe, g)
            pe.wait_ge(stackT_ready, 4)
            pe.wait_ge(hidden_ready, 8)
            pe.wait_ge(sumsT_ready, NG)
            max_pe(pe, 0)
            pe.wait_ge(h_ready, NG)
            max_pe(pe, 1)
            max_pe(pe, 2)
            turn_pe(pe, turn_at("h", NG - 1), y, NG - 1, hn_ready, NG)
            max_pe(pe, 3)
            keys_pe(pe, NG - 1)
            stack_pe(pe, 2)
            for n in range(4, EARLY):
                max_pe(pe, n)
            stack_pe(pe, NG - 1)
            pe.wait_ge(stackT_ready, 2 * NG)
            pe.wait_ge(hidden_ready, 4 * (NG - 1))
            for n in range(EARLY, 2 * NT):
                max_pe(pe, n)
            for g in range(NG):
                pe.wait_ge(rowmax_ready, maxima(2 * NT - 2 + g // 2))
                for q in range(GT):
                    last = pe.transpose(turned_max(g)[:, q * PART:(q + 1) * PART],
                                        row_max[:, g, q * PART:(q + 1) * PART], identh[:, :])
                last.then_inc(rowmax_turned, 1)
            for g in range(2):
                pe.wait_ge(m_step, 5)
                turn_stack_pe(pe, 2 + g, g, k_stack).then_inc(mT_done, 1)
            total = NG * NT // 2
            for n in range(total + BEHIND):
                begins = n > BEHIND and (n - BEHIND) % (NT // 2) == 0
                after = n > BEHIND + 1 and (n - BEHIND) % (NT // 2) == 1
                if n < total and not after:
                    pair_scores_pe(pe, n)
                if n == 1:
                    for g in range(2, NG):
                        pe.wait_ge(m_step, 10)
                        turn_stack_pe(pe, 2 + g, g, k_stack).then_inc(mT_done, 1)
                if begins and n + 1 < total:
                    pair_scores_pe(pe, n + 1)
                if n >= BEHIND:
                    first_product_pe(pe, n - BEHIND)
            for n in range(1, 4):
                for g in range(NG):
                    k = n * NG + g
                    pe.wait_ge(va_read, max(k - 1, NG))
                    for jt in range(NT):
                        if g == 0 and jt % GT == 0:
                            pe.wait_ge(va_ready, (n - 1) * NG + jt // GT + 1)
                        for q in range(GT):
                            for a in range(2):
                                last = pe.matmul(product_sums(k, q), prob16[:, g, jt, a, q * PART:(q + 1) * PART],
                                                 val16[:, (n + 1) % 2, jt, 0:HALF], start=(q == 0 and jt == 0 and a == 0),
                                                 stop=(jt == NT - 1 and a == 1), skip_group_check=True)
                        if n == 3 and g > 0 and jt == 11:
                            turn_rows_pe(pe, 1, g - 1)
                        if n == 3 and g > 0 and jt == 14:
                            inputs_pe(pe, 1, g - 1)
                    last.then_inc(va_done, 1)

        def scores_pe(pe, to, jt, g, rows):
            pe.matmul(to, hide[:, :], hidden[:, g, jt, :], start=True, stop=False)
            return pe.matmul(to, qT[0:rows, jt // GT, (jt % GT) * PART:(jt % GT + 1) * PART], kT[0:rows, g, :],
                             start=False, stop=True)

        @block.tensor
        def _(pe):
            pe.wait_ge(consts_ready, 1)
            for n in range(8):
                pe.matmul(psum[:, 3, 0:PART], ones[:, :], ones[:, :], start=True, stop=True)
            pe.wait_ge(ident_ready, 1)
            pe.wait_ge(x_loaded, 16)
            for g in range(NG):
                turn_pe(pe, turn_at(0, g), x, g, x_loaded, 16)
            pe.wait_ge(arep_ready, 1)
            pe.wait_ge(w_loaded, 16)
            for al in range(NL):
                last = pe.matmul(psum[0:F, al, 0:PART + 2], wts[:, al * LW + F:al * LW + 2 * F], a_rep[al],
                                 start=True, stop=True)
            last.then_inc(wa_done, 1)
            pe.wait_ge(wcopy_ready, 2 * NL)
            for g in range(NG):
                wh_pe(pe, 0, g)
            pe.wait_ge(wsq_ready, 1)
            pe.wait_ge(consts_ready, 1)
            pe.wait_ge(xT_ready, NG)
            pe.matmul(psum[:, MISC, 256:256 + NL - 1], ones[:, :], w_dst2[:, 1:NL], start=True,
                      stop=True).then_inc(wnorm_done, 1)
            pe.wait_ge(dmax_part, 1)
            pe.wait_ge(wnorm_ready, 1)
            pe.transpose(psum[0:1, MISC, 0:PART], dmax[:, :], ident[:, :]).then_inc(dmax_turned, 1)
            src_pe(pe, 0, 0)
            pe.wait_ge(dmax_one, 1)
            pe.matmul(psum[:, MISC, 384:385], ones[0:1, :], dmax1[:, :], start=True, stop=True).then_inc(dmax_spread, 1)
            src_pe(pe, 0, 1)
            src_pe(pe, 0, 2)
            pe.wait_ge(dmax_ready, 1)
            src_pe(pe, 0, 3)
            for al in range(NL):
                for g in range(NG):
                    group_sums_pe(pe, al, g)
                if al == 0:
                    layer1_pe(pe)


def kernel(x, adj, L0_gnn_W, L0_gnn_a, L1_gnn_w_k, L1_gnn_w_q, L2_gnn_W, L2_gnn_a, L3_gnn_W, L3_gnn_a):
    import numpy as np
    import concourse.bacc as bacc
    from concourse import mybir as _mybir
    from concourse.bass_utils import run_bass_kernel_spmd

    n, f = x.shape
    part, group = 128, 512
    x_rows = np.ascontiguousarray(np.asarray(x).reshape(n // part, part, f).transpose(1, 0, 2)).reshape(part, -1)
    adj_t = np.ascontiguousarray(np.asarray(adj).T.reshape(n // part, part, n // group, group).transpose(2, 1, 0, 3))
    adj_t = adj_t.reshape(n // group, part, -1)
    columns = []
    for w, a in ((L0_gnn_W, L0_gnn_a), (L2_gnn_W, L2_gnn_a), (L3_gnn_W, L3_gnn_a)):
        w, a = np.asarray(w), np.asarray(a)
        columns += [w, w.T, a.reshape(2, f).T]
    weights = np.ascontiguousarray(np.concatenate(columns + [np.asarray(L1_gnn_w_k), np.asarray(L1_gnn_w_q)], axis=1))

    nc = bacc.Bacc("TRN2", target_bir_lowering=False, num_devices=1, dynamic_dma_scratch_size=4096)
    arrays = {"x_rows": x_rows, "adj_t": adj_t, "weights": weights}
    args = [nc.dram_tensor(name, a.shape, _mybir.dt.from_np(a.dtype), kind="ExternalInput").ap()
            for name, a in arrays.items()]
    out = nc.dram_tensor("out_rows", x_rows.shape, _mybir.dt.float32, kind="ExternalOutput").ap()
    graph_layers(nc, *args, out, slopes=(0.2, 0.2, 0.01))
    got = run_bass_kernel_spmd(nc, [arrays], core_ids=[0]).results[0]["out_rows"]
    return np.ascontiguousarray(np.asarray(got).reshape(part, n // part, f).transpose(1, 0, 2)).reshape(n, f)
```
